# Optimizing a Trainium2 kernel written in Bass

```python
import numpy as np
import jax
import jax.numpy as jnp

def _softmax(x, axis=-1):
    return jax.nn.softmax(x, axis=axis)

def _gelu(x):
    return jax.nn.gelu(x, approximate=True)

def _silu(x):
    return jax.nn.silu(x)

def _sigmoid(x):
    return jax.nn.sigmoid(x)

def _layernorm(x, axis=-1, eps=1e-05):
    m = jnp.mean(x, axis=axis, keepdims=True)
    v = jnp.var(x, axis=axis, keepdims=True)
    return (x - m) / jnp.sqrt(v + eps)

def _scatter_add(tgt, idx, src, axis=0):
    return tgt.at[idx].add(src)

def _segment_sum(src, seg, n):
    return jax.ops.segment_sum(src, seg, n)
kernel_name = 'mk_seq_postln_d2_jaxref_r4_9bc4da'

def setup_inputs(seed: int=0):
    np.random.seed(seed)
    _w = jnp.asarray

    def _L0_attn_setup():
        import jax, jax.numpy as jnp
        import numpy as np
        BLOCK_H = 32
        BLOCK_W = 32
        N_FEAT = 1024
        K_FEAT = 1024
        key = jax.random.key(seed)
        k1, k2, k3 = jax.random.split(key, 3)
        data = jax.random.normal(k1, (4, 256, K_FEAT), dtype=jnp.float32)
        weight = jax.random.normal(k2, (N_FEAT, K_FEAT), dtype=jnp.float32) * 0.02
        nb, kb = (N_FEAT // BLOCK_H, K_FEAT // BLOCK_W)
        block_pattern = jax.random.randint(k3, (nb, kb), 0, 2, dtype=jnp.int32)
        mask = jnp.repeat(jnp.repeat(block_pattern, BLOCK_H, axis=0), BLOCK_W, axis=1)
        return {'data': data, 'weight': weight, 'mask': mask}
    _L0_attn_in = _L0_attn_setup()

    def _L0_ffn_setup():
        import jax, jax.numpy as jnp
        import numpy as np
        LORA_RANK = 16
        LORA_ALPHA = 16
        LORA_SCALE = LORA_ALPHA / LORA_RANK
        key = jax.random.key(seed)
        k1, k2, k3, k4, k5 = jax.random.split(key, 5)
        B, S, D_IN, D_OUT, N_LORA, R = (8, 512, 1024, 1024, 3, LORA_RANK)
        std = 1.0 / np.sqrt(D_IN)
        x = jax.random.normal(k1, (B, S, D_IN), dtype=jnp.float32)
        weight = jax.random.truncated_normal(k2, -3.0, 3.0, (D_OUT, D_IN), dtype=jnp.float32) * std
        bias = jax.random.normal(k3, (D_OUT,), dtype=jnp.float32) * 0.01
        lora_A = jax.random.normal(k4, (N_LORA, R, D_IN), dtype=jnp.float32) * std
        lora_B = jax.random.normal(k5, (N_LORA, D_OUT, R), dtype=jnp.float32) * 0.02
        lora_start_indices = jnp.arange(4, dtype=jnp.int64) * 2
        return {'x': x, 'weight': weight, 'bias': bias, 'lora_A': lora_A, 'lora_B': lora_B, 'lora_start_indices': lora_start_indices}
    _L0_ffn_in = _L0_ffn_setup()

    def _L1_attn_setup():
        import jax, jax.numpy as jnp
        import numpy as np
        DEPTH, DIM, DFF, VOCAB = (4, 128, 512, 1024)
        EPS = 1e-05

        def layernorm(x, w, b):
            mu = jnp.mean(x, axis=-1, keepdims=True)
            var = jnp.mean((x - mu) ** 2, axis=-1, keepdims=True)
            return (x - mu) * jax.lax.rsqrt(var + EPS) * w + b

        def sconv(x, phazor_c, last_conv_c):
            B, L, D = x.shape
            r = jnp.abs(phazor_c)
            p = jnp.tanh(r) * jnp.exp(1j * jnp.angle(phazor_c))
            prog = p[None, :] ** jnp.arange(L, dtype=jnp.float32)[:, None]
            filt_fft = jnp.fft.fft(prog, n=2 * L, axis=0)
            x_fft = jnp.fft.fft(x.astype(jnp.complex64), n=2 * L, axis=1)
            conv = jnp.fft.ifft(filt_fft[None] * x_fft, axis=1)[:, :L]
            conv = conv + last_conv_c[None, None, :] * prog[None] * p[None, None, :]
            return conv.real.astype(x.dtype)

        def _forward(x, Win, bin, ln1_w, ln1_b, phz_re, phz_im, lc_re, lc_im, sc_lin, ln2_w, ln2_b, W1, b1, W2, b2, lnl_w, lnl_b, Wout, bout):
            h = jnp.einsum('blv,dv->bld', x, Win) + bin

            def body(h, p):
                l1w, l1b, pr, pi, lr, li, scl, l2w, l2b, w1, b1_, w2, b2_ = p
                y = jax.nn.silu(layernorm(h, l1w, l1b))
                y = sconv(y, pr + 1j * pi, lr + 1j * li)
                h = h + y * scl
                y = layernorm(h, l2w, l2b)
                y = jax.nn.silu(jnp.einsum('bld,fd->blf', y, w1) + b1_)
                y = jnp.einsum('blf,df->bld', y, w2) + b2_
                return (h + y, None)
            xs = (ln1_w, ln1_b, phz_re, phz_im, lc_re, lc_im, sc_lin, ln2_w, ln2_b, W1, b1, W2, b2)
            h, _ = jax.lax.scan(body, h, xs)
            h = layernorm(h, lnl_w, lnl_b)
            return jnp.einsum('bld,vd->blv', h, Wout) + bout
        key = jax.random.key(seed)
        ks = jax.random.split(key, 20)
        f32 = jnp.float32
        inp = {}
        inp['x'] = jax.random.normal(ks[0], (2, 1024, VOCAB), dtype=f32)
        inp['Win'] = jax.random.normal(ks[1], (DIM, VOCAB), dtype=f32) * VOCAB ** (-0.5)
        inp['bin'] = jnp.zeros((DIM,), f32)
        inp['ln1_w'] = jnp.ones((DEPTH, DIM), f32)
        inp['ln1_b'] = jnp.zeros((DEPTH, DIM), f32)
        ang = 2 * np.pi * jnp.arange(DIM, dtype=f32) / DIM
        mag = jnp.abs(jax.random.normal(ks[2], (DEPTH, DIM), dtype=f32))
        inp['phz_re'] = mag * jnp.cos(ang)[None]
        inp['phz_im'] = mag * jnp.sin(ang)[None]
        inp['lc_re'] = jax.random.normal(ks[3], (DEPTH, DIM), dtype=f32)
        inp['lc_im'] = jax.random.normal(ks[4], (DEPTH, DIM), dtype=f32)
        inp['sc_lin'] = jnp.ones((DEPTH, DIM), f32)
        inp['ln2_w'] = jnp.ones((DEPTH, DIM), f32)
        inp['ln2_b'] = jnp.zeros((DEPTH, DIM), f32)
        inp['W1'] = jax.random.normal(ks[5], (DEPTH, DFF, DIM), dtype=f32) * DIM ** (-0.5)
        inp['b1'] = jnp.zeros((DEPTH, DFF), f32)
        inp['W2'] = jax.random.normal(ks[6], (DEPTH, DIM, DFF), dtype=f32) * DFF ** (-0.5)
        inp['b2'] = jnp.zeros((DEPTH, DIM), f32)
        inp['lnl_w'] = jnp.ones((DIM,), f32)
        inp['lnl_b'] = jnp.zeros((DIM,), f32)
        inp['Wout'] = jax.random.normal(ks[7], (VOCAB, DIM), dtype=f32) * DIM ** (-0.5)
        inp['bout'] = jnp.zeros((VOCAB,), f32)
        return inp
    _L1_attn_in = _L1_attn_setup()

    def _L1_ffn_setup():
        import jax, jax.numpy as jnp
        import numpy as np
        IMAGE_START_POS = 34
        Q_START = IMAGE_START_POS + 144 + 1
        Q_END = -1
        LORA_ALPHA = 32
        LORA_RANK = 16
        SCALING = LORA_ALPHA / LORA_RANK
        key = jax.random.key(seed)
        ks = jax.random.split(key, 7)
        B_, S, D, O, E, R = (4, 512, 1024, 1024, 8, LORA_RANK)
        s = 0.02
        return {'x': jax.random.normal(ks[0], (B_, S, D), jnp.float32), 'W': jax.random.normal(ks[1], (O, D), jnp.float32) * s, 'b': jax.random.normal(ks[2], (O,), jnp.float32) * s, 'A': jax.random.normal(ks[3], (E, R, D), jnp.float32) * s, 'B': jax.random.normal(ks[4], (E, O, R), jnp.float32) * s, 'router_W': jax.random.normal(ks[5], (E, D), jnp.float32) * s, 'router_b': jax.random.normal(ks[6], (E,), jnp.float32) * s}
    _L1_ffn_in = _L1_ffn_setup()
    _d = {'L0_attn_data': _L0_attn_in['data'], 'L0_attn_weight': _L0_attn_in['weight'], 'L0_attn_mask': _L0_attn_in['mask'], 'L0_ffn_weight': _L0_ffn_in['weight'], 'L0_ffn_bias': _L0_ffn_in['bias'], 'L0_ffn_lora_A': _L0_ffn_in['lora_A'], 'L0_ffn_lora_B': _L0_ffn_in['lora_B'], 'L0_ffn_lora_start_indices': _L0_ffn_in['lora_start_indices'], 'L1_attn_Win': _L1_attn_in['Win'], 'L1_attn_bin': _L1_attn_in['bin'], 'L1_attn_ln1_w': _L1_attn_in['ln1_w'], 'L1_attn_ln1_b': _L1_attn_in['ln1_b'], 'L1_attn_phz_re': _L1_attn_in['phz_re'], 'L1_attn_phz_im': _L1_attn_in['phz_im'], 'L1_attn_lc_re': _L1_attn_in['lc_re'], 'L1_attn_lc_im': _L1_attn_in['lc_im'], 'L1_attn_sc_lin': _L1_attn_in['sc_lin'], 'L1_attn_ln2_w': _L1_attn_in['ln2_w'], 'L1_attn_ln2_b': _L1_attn_in['ln2_b'], 'L1_attn_W1': _L1_attn_in['W1'], 'L1_attn_b1': _L1_attn_in['b1'], 'L1_attn_W2': _L1_attn_in['W2'], 'L1_attn_b2': _L1_attn_in['b2'], 'L1_attn_lnl_w': _L1_attn_in['lnl_w'], 'L1_attn_lnl_b': _L1_attn_in['lnl_b'], 'L1_attn_Wout': _L1_attn_in['Wout'], 'L1_attn_bout': _L1_attn_in['bout'], 'L1_ffn_W': _L1_ffn_in['W'], 'L1_ffn_b': _L1_ffn_in['b'], 'L1_ffn_A': _L1_ffn_in['A'], 'L1_ffn_B': _L1_ffn_in['B'], 'L1_ffn_router_W': _L1_ffn_in['router_W'], 'L1_ffn_router_b': _L1_ffn_in['router_b']}
    _x0 = _d['L0_attn_data']
    _d['L0_attn_data'] = jax.random.normal(jax.random.fold_in(jax.random.key(seed), 1), (4, 1024, 1024), dtype=_x0.dtype)
    del _x0
    return _d

def reference(L0_attn_data, L0_attn_weight, L0_attn_mask, L0_ffn_weight, L0_ffn_bias, L0_ffn_lora_A, L0_ffn_lora_B, L0_ffn_lora_start_indices, L1_attn_Win, L1_attn_bin, L1_attn_ln1_w, L1_attn_ln1_b, L1_attn_phz_re, L1_attn_phz_im, L1_attn_lc_re, L1_attn_lc_im, L1_attn_sc_lin, L1_attn_ln2_w, L1_attn_ln2_b, L1_attn_W1, L1_attn_b1, L1_attn_W2, L1_attn_b2, L1_attn_lnl_w, L1_attn_lnl_b, L1_attn_Wout, L1_attn_bout, L1_ffn_W, L1_ffn_b, L1_ffn_A, L1_ffn_B, L1_ffn_router_W, L1_ffn_router_b):

    def _L0_attn_ref(data, weight, mask):
        import jax, jax.numpy as jnp
        import numpy as np
        BLOCK_H = 32
        BLOCK_W = 32
        N_FEAT = 1024
        K_FEAT = 1024
        N, K = weight.shape
        nb, kb = (N // BLOCK_H, K // BLOCK_W)
        block_mask = mask.reshape(nb, BLOCK_H, kb, BLOCK_W).astype(jnp.float32).sum(axis=(1, 3)) > 0
        elem_mask = jnp.repeat(jnp.repeat(block_mask, BLOCK_H, axis=0), BLOCK_W, axis=1)
        w_masked = weight * elem_mask.astype(weight.dtype)
        out = jnp.einsum('bsk,nk->bsn', data, w_masked)
        return out

    def _L0_ffn_ref(x, weight, bias, lora_A, lora_B, lora_start_indices):
        import jax, jax.numpy as jnp
        import numpy as np
        LORA_RANK = 16
        LORA_ALPHA = 16
        LORA_SCALE = LORA_ALPHA / LORA_RANK
        y = jnp.einsum('bsd,od->bso', x, weight) + bias
        B = x.shape[0]
        seg = jnp.searchsorted(lora_start_indices, jnp.arange(B), side='right') - 1
        adapter_idx = jnp.clip(seg - 1, 0, lora_A.shape[0] - 1)
        A = lora_A[adapter_idx]
        Bw = lora_B[adapter_idx]
        lo = jnp.einsum('bsr,bor->bso', jnp.einsum('bsd,brd->bsr', x, A), Bw) * LORA_SCALE
        use_lora = (seg > 0)[:, None, None]
        return y + jnp.where(use_lora, lo, jnp.zeros((), dtype=y.dtype))

    def _L1_attn_ref(x, Win, bin, ln1_w, ln1_b, phz_re, phz_im, lc_re, lc_im, sc_lin, ln2_w, ln2_b, W1, b1, W2, b2, lnl_w, lnl_b, Wout, bout):
        import jax, jax.numpy as jnp
        import numpy as np
        DEPTH, DIM, DFF, VOCAB = (4, 128, 512, 1024)
        EPS = 1e-05

        def layernorm(x, w, b):
            mu = jnp.mean(x, axis=-1, keepdims=True)
            var = jnp.mean((x - mu) ** 2, axis=-1, keepdims=True)
            return (x - mu) * jax.lax.rsqrt(var + EPS) * w + b

        def sconv(x, phazor_c, last_conv_c):
            B, L, D = x.shape
            r = jnp.abs(phazor_c)
            p = jnp.tanh(r) * jnp.exp(1j * jnp.angle(phazor_c))
            prog = p[None, :] ** jnp.arange(L, dtype=jnp.float32)[:, None]
            filt_fft = jnp.fft.fft(prog, n=2 * L, axis=0)
            x_fft = jnp.fft.fft(x.astype(jnp.complex64), n=2 * L, axis=1)
            conv = jnp.fft.ifft(filt_fft[None] * x_fft, axis=1)[:, :L]
            conv = conv + last_conv_c[None, None, :] * prog[None] * p[None, None, :]
            return conv.real.astype(x.dtype)

        def _forward(x, Win, bin, ln1_w, ln1_b, phz_re, phz_im, lc_re, lc_im, sc_lin, ln2_w, ln2_b, W1, b1, W2, b2, lnl_w, lnl_b, Wout, bout):
            h = jnp.einsum('blv,dv->bld', x, Win) + bin

            def body(h, p):
                l1w, l1b, pr, pi, lr, li, scl, l2w, l2b, w1, b1_, w2, b2_ = p
                y = jax.nn.silu(layernorm(h, l1w, l1b))
                y = sconv(y, pr + 1j * pi, lr + 1j * li)
                h = h + y * scl
                y = layernorm(h, l2w, l2b)
                y = jax.nn.silu(jnp.einsum('bld,fd->blf', y, w1) + b1_)
                y = jnp.einsum('blf,df->bld', y, w2) + b2_
                return (h + y, None)
            xs = (ln1_w, ln1_b, phz_re, phz_im, lc_re, lc_im, sc_lin, ln2_w, ln2_b, W1, b1, W2, b2)
            h, _ = jax.lax.scan(body, h, xs)
            h = layernorm(h, lnl_w, lnl_b)
            return jnp.einsum('bld,vd->blv', h, Wout) + bout
        return _forward(x, Win, bin, ln1_w, ln1_b, phz_re, phz_im, lc_re, lc_im, sc_lin, ln2_w, ln2_b, W1, b1, W2, b2, lnl_w, lnl_b, Wout, bout)

    def _L1_ffn_ref(x, W, b, A, B, router_W, router_b):
        import jax, jax.numpy as jnp
        import numpy as np
        IMAGE_START_POS = 34
        Q_START = IMAGE_START_POS + 144 + 1
        Q_END = -1
        LORA_ALPHA = 32
        LORA_RANK = 16
        SCALING = LORA_ALPHA / LORA_RANK
        x_q = x[:, Q_START:Q_END, :]
        q = x_q.mean(axis=1)
        logits = q @ router_W.T + router_b
        routing = jax.nn.softmax(logits, axis=-1)
        base = x @ W.T + b
        t = jnp.einsum('bsd,erd->bser', x, A)
        lora = jnp.einsum('bser,eor,be->bso', t, B, routing) * SCALING
        return base + lora
    x = L0_attn_data
    x = _layernorm(x + _L0_attn_ref(x, L0_attn_weight, L0_attn_mask), axis=-1)
    x = _layernorm(x + _L0_ffn_ref(x, L0_ffn_weight, L0_ffn_bias, L0_ffn_lora_A, L0_ffn_lora_B, L0_ffn_lora_start_indices), axis=-1)
    x = _layernorm(x + _L1_attn_ref(x, L1_attn_Win, L1_attn_bin, L1_attn_ln1_w, L1_attn_ln1_b, L1_attn_phz_re, L1_attn_phz_im, L1_attn_lc_re, L1_attn_lc_im, L1_attn_sc_lin, L1_attn_ln2_w, L1_attn_ln2_b, L1_attn_W1, L1_attn_b1, L1_attn_W2, L1_attn_b2, L1_attn_lnl_w, L1_attn_lnl_b, L1_attn_Wout, L1_attn_bout), axis=-1)
    x = _layernorm(x + _L1_ffn_ref(x, L1_ffn_W, L1_ffn_b, L1_ffn_A, L1_ffn_B, L1_ffn_router_W, L1_ffn_router_b), axis=-1)
    return x

_drawn_inputs = setup_inputs


def setup_inputs(seed=0):
    import zlib

    import numpy as np

    out = dict(_drawn_inputs(seed))
    spreads = {'L1_attn_bin': (0.0, 0.1),
     'L1_attn_ln1_w': (1.0, 0.2),
     'L1_attn_ln1_b': (0.0, 0.1),
     'L1_attn_sc_lin': (1.0, 0.2),
     'L1_attn_ln2_w': (1.0, 0.2),
     'L1_attn_ln2_b': (0.0, 0.458),
     'L1_attn_b1': (0.0, 0.268),
     'L1_attn_b2': (0.0, 0.1),
     'L1_attn_lnl_w': (1.0, 0.2),
     'L1_attn_lnl_b': (0.0, 0.1),
     'L1_attn_bout': (0.0, 0.1)}
    factors = {'L0_ffn_bias': 4.804,
     'L1_attn_lc_im': 2.891,
     'L1_ffn_b': 3.719,
     'L1_ffn_router_W': 4.211,
     'L1_ffn_router_b': 64.0}
    for name, (base, spread) in spreads.items():
        noise = np.random.default_rng([zlib.crc32(name.encode()), seed]).standard_normal(out[name].shape)
        drawn = base * np.exp(spread * noise) if base else spread * noise
        out[name] = jnp.asarray(drawn.astype(out[name].dtype))
    for name, factor in factors.items():
        out[name] = (out[name] * factor).astype(out[name].dtype)
    return out
```

```python
from contextlib import ExitStack, nullcontext

import concourse.bass as bass
from concourse import mybir

P = 128
D = 1024
KC = D // P
HALF = 512
BATCHES = 4
SEQ = 1024
TILES = BATCHES * SEQ // P
TPB = SEQ // P
BODY = 2 * TPB
EPS = 1e-5
LAYERS = 4
FCH = 4
UNITS = BATCHES * SEQ // HALF
EXPERTS = 8
ROUTER_SCALE = 2.0
ROUTED_START = 34 + 144 + 1
ROUTED_END = SEQ - 1

F32 = mybir.dt.float32
F32R = mybir.dt.float32r
I32 = mybir.dt.int32
ALU = mybir.AluOpType
ACT = mybir.ActivationFunctionType
AX = mybir.AxisListType.X


def dense_phase(nc, kind, io, wall, ident):
    low_rank = kind in "BD"
    project = kind == "B"
    rank = io["rank"] if low_rank else 0
    with ExitStack() as ctx:
        def sb(name, shape, dt=F32):
            return ctx.enter_context(nc.sbuf_tensor(f"{kind}_{name}", shape, dt))

        def psum(name, shape):
            return ctx.enter_context(nc.psum_tensor(f"{kind}_{name}", shape, F32))

        def sem(name):
            return ctx.enter_context(nc.semaphore(f"{kind}_{name}"))

        x_in = sb("x_in", [P, D])
        x_hi = sb("x_hi", [P, 2, KC, P], F32R)
        x_lo = sb("x_lo", [P, 2, KC, P], F32R)
        row = sb("row", [P, 2, D])
        stats = sb("stats", [P, 2, 2, 6])
        mean_var = sb("mean_var", [P, 2, 2])
        var_eps = sb("var_eps", [P, 2])
        rstd = sb("rstd", [P, 2])
        shift = sb("shift", [P, 2])
        minus_half = sb("minus_half", [P, 1])
        ps_out = [psum(f"ps_out{h}", [P, HALF]) for h in range(2)]
        if low_rank:
            bias = sb("bias", [P, D])
            a_in = sb("a_in", [rank, P])
            a_hi = sb("a_hi", [rank, P], F32R)
            a_lo = sb("a_lo", [rank, P], F32R)
            b_hi = sb("b_hi", [rank, D], F32R)
            b_lo = sb("b_lo", [rank, D], F32R)
            w_in = sb("w_in", [P, 2, HALF])
            ps_x = psum("ps_x", [P, D])
            ps_w = psum("ps_w", [P, HALF])
        if project:
            y_hi = sb("y_hi", [P, KC, 2 * P], F32R)
            y_lo = sb("y_lo", [P, KC, 2 * P], F32R)
            h_out = sb("h_out", [P, 2, 2 * P])
            ps_y = psum("ps_y", [P, D])
            ps_h = psum("ps_h", [P, 2 * P])

        x_loaded = sem("x_loaded")
        x_turned = sem("x_turned")
        hi_ready = sem("hi_ready")
        lo_ready = sem("lo_ready")
        mm_done = sem("mm_done")
        evacuated = [sem(f"evacuated{h}") for h in range(2)]
        stats_ready = sem("stats_ready")
        mv_ready = sem("mv_ready")
        ve_ready = sem("ve_ready")
        rstd_ready = sem("rstd_ready")
        shift_ready = sem("shift_ready")
        normed = sem("normed")
        stored = [sem(f"stored{s}") for s in range(2)]
        const_ready = sem("const_ready")
        bias_loaded = sem("bias_loaded")
        a_loaded = sem("a_loaded")
        a_hi_ready = sem("a_hi_ready")
        a_lo_ready = sem("a_lo_ready")
        bt_loaded = sem("bt_loaded")
        bs_scaled = sem("bs_scaled")
        b_hi_ready = sem("b_hi_ready")
        b_lo_ready = sem("b_lo_ready")
        w_loaded = [sem(f"w_loaded{o}") for o in range(2)]
        w_diag = sem("w_diag")
        w_product = sem("w_product")
        w_summed = sem("w_summed")
        w_hi_ready = sem("w_hi_ready")
        w_lo_ready = sem("w_lo_ready")
        y_turned = sem("y_turned")
        y_hi_ready = sem("y_hi_ready")
        y_lo_ready = sem("y_lo_ready")
        h_done = sem("h_done")
        h_evacuated = sem("h_evacuated")
        h_stored = [sem(f"h_stored{s}") for s in range(2)]

        def steps(eng, step):
            with eng.Fori(0, TILES // BODY) as turn:
                for j in range(BODY):
                    step(turn, j)

        def only_in(eng, which, guarded, turn):
            return (eng.If(turn < 1 if which == 0 else turn > 0), which) if guarded else (nullcontext(), turn)

        def unit(batch, k, o):
            return 2 * KC * batch + 2 * k + o

        def weights_next(eng, turn, j, part):
            if low_rank:
                guard, now = only_in(eng, 0, j >= TPB, turn)
                with guard:
                    part(2 * now + j // TPB + 1, (j // TPB + 1) % 2, j % TPB)

        block = ctx.enter_context(nc.Block())

        @block.sync
        def _(sp):
            def load_x(t):
                if low_rank:
                    sp.wait_ge(x_turned, t)
                else:
                    sp.wait_ge(hi_ready, t)
                    sp.wait_ge(lo_ready, t)
                sp.dma_start(x_in[:], io["x"][t]).then_inc(x_loaded, 16)

            def load_b(batch):
                for o in range(2):
                    sp.wait_ge(w_hi_ready, 2 * KC * batch)
                    sp.wait_ge(w_lo_ready, 2 * KC * batch)
                    sp.dma_start(w_in[:rank, o], io["b_t"][:, o * HALF:(o + 1) * HALF]).then_inc(bt_loaded, 16)

            def load_w(batch, par, k):
                if k == 0:
                    load_b(batch)
                sp.wait_ge(a_hi_ready, KC * batch + k)
                sp.wait_ge(a_lo_ready, KC * batch + k)
                sp.dma_start(a_in[:], io["a"][:, k * P:(k + 1) * P]).then_inc(a_loaded, 16)
                if k == 0:
                    sp.wait_ge(b_hi_ready, 2 * batch + 2)
                    sp.wait_ge(b_lo_ready, 2 * batch + 2)
                for o in range(2):
                    if k > 0:
                        sp.wait_ge(w_hi_ready, unit(batch, k - 1, o) + 1)
                        sp.wait_ge(w_lo_ready, unit(batch, k - 1, o) + 1)
                    sp.dma_start(w_in[:, o], io["w"][k][:, o * HALF:(o + 1) * HALF]).then_inc(w_loaded[o], 16)

            load_x(0)
            if low_rank:
                sp.dma_start(bias[:], io["bias"].partition_broadcast(P)).then_inc(bias_loaded, 16)
                for k in range(KC):
                    load_w(0, 0, k)
            load_x(1)

            def step(turn, j):
                weights_next(sp, turn, j, load_w)
                guard, now = only_in(sp, 0, j >= BODY - 2, turn)
                with guard:
                    load_x(BODY * now + j + 2)

            steps(sp, step)

        @block.tensor
        def _(pe):
            def turn_x(t):
                pe.wait_ge(x_loaded, 16 * (t + 1))
                pe.wait_ge(hi_ready, t)
                pe.wait_ge(lo_ready, t)
                for k in range(KC):
                    last = pe.transpose(ps_x[:, k * P:(k + 1) * P], x_in[:, k * P:(k + 1) * P], ident[:])
                last.then_inc(x_turned, 1)

            def product(t, j, par, h):
                if h == 0:
                    pe.wait_ge(hi_ready, t + 1)
                    pe.wait_ge(lo_ready, t + 1)
                pe.wait_ge(evacuated[h], t)
                cols = slice(h * HALF, (h + 1) * HALF)
                s = j % 2
                for k in range(KC):
                    pe.matmul(ps_out[h][:], x_hi[:, s, k], wall[:, par, 0, k, cols], start=(k == 0), stop=False)
                    pe.matmul(ps_out[h][:], x_hi[:, s, k], wall[:, par, 1, k, cols], start=False, stop=False)
                    last = pe.matmul(ps_out[h][:], x_lo[:, s, k], wall[:, par, 0, k, cols],
                                     start=False, stop=(k == KC - 1))
                last.then_inc(mm_done, 1)

            def weight_part(batch, k, o):
                n = unit(batch, k, o)
                pe.wait_ge(a_hi_ready, KC * batch + k + 1)
                pe.wait_ge(a_lo_ready, KC * batch + k + 1)
                pe.wait_ge(b_hi_ready, 2 * batch + 2)
                pe.wait_ge(b_lo_ready, 2 * batch + 2)
                pe.wait_ge(w_summed, n)
                cols = slice(o * HALF, (o + 1) * HALF)
                pe.matmul(ps_w[:], a_hi[:], b_hi[:, cols], start=True, stop=False)
                pe.matmul(ps_w[:], a_hi[:], b_lo[:, cols], start=False, stop=False)
                pe.matmul(ps_w[:], a_lo[:], b_hi[:, cols], start=False, stop=True).then_inc(w_product, 1)

            def turn_y(t, j):
                pe.wait_ge(normed, t + 1)
                pe.wait_ge(y_hi_ready, t + 1)
                pe.wait_ge(y_lo_ready, t + 1)
                for k in range(KC):
                    last = pe.transpose(ps_y[:, k * P:(k + 1) * P], row[:, j % 2, k * P:(k + 1) * P], ident[:])
                last.then_inc(y_turned, 1)

            def project_pair(pair):
                pe.wait_ge(y_hi_ready, 2 * pair + 3)
                pe.wait_ge(y_lo_ready, 2 * pair + 3)
                pe.wait_ge(h_evacuated, pair + 1)
                for k in range(KC):
                    pe.matmul(ps_h[:], io["win_hi"][:, k], y_hi[:, k], start=(k == 0), stop=False)
                    pe.matmul(ps_h[:], io["win_hi"][:, k], y_lo[:, k], start=False, stop=False)
                    last = pe.matmul(ps_h[:], io["win_lo"][:, k], y_hi[:, k], start=False, stop=(k == KC - 1))
                last.then_inc(h_done, 1)

            if low_rank:
                turn_x(0)
                for k in range(KC):
                    for o in range(2):
                        weight_part(0, k, o)

            def step(turn, j):
                t = BODY * turn + j
                batch = 2 * turn + j // TPB
                if low_rank:
                    guard, now = only_in(pe, 0, j == BODY - 1, turn)
                    with guard:
                        turn_x(BODY * now + j + 1)
                    if j % TPB == 0:
                        pe.wait_ge(w_hi_ready, 2 * KC * (batch + 1))
                        pe.wait_ge(w_lo_ready, 2 * KC * (batch + 1))
                par = (j // TPB) % 2 if low_rank else 1
                product(t, j, par, 0)
                if project and j % 2:
                    guard, now = only_in(pe, 1, j == 1, turn)
                    with guard:
                        project_pair(TPB * now + (j - 3) // 2)
                weights_next(pe, turn, j, lambda batch, par, k: weight_part(batch, k, 0))
                product(t, j, par, 1)
                weights_next(pe, turn, j, lambda batch, par, k: weight_part(batch, k, 1))
                if project:
                    guard, now = only_in(pe, 1, j == 0, turn)
                    with guard:
                        turn_y(BODY * now + j - 1, j + 1)

            steps(pe, step)
            if project:
                turn_y(TILES - 1, 1)
                project_pair(TILES // 2 - 1)

        @block.scalar
        def _(act):
            def split_x(t, j):
                if low_rank:
                    act.wait_ge(x_turned, t + 1)
                else:
                    act.wait_ge(x_loaded, 16 * (t + 1))
                if not (isinstance(t, int) and t < 2):
                    act.wait_ge(mm_done, 2 * (t - 1))
                src = ps_x if low_rank else x_in
                act.activation(x_hi[:, j % 2].rearrange("p k t -> p (k t)"), src[:], ACT.Identity)\
                   .then_inc(hi_ready, 1)

            def split_a(batch, k):
                act.wait_ge(a_loaded, 16 * (KC * batch + k + 1))
                act.wait_ge(w_product, unit(batch, k, 0))
                act.activation(a_hi[:], a_in[:], ACT.Identity).then_inc(a_hi_ready, 1)

            def split_b(batch):
                for o in range(2):
                    act.wait_ge(bs_scaled, 2 * batch + o + 1)
                    act.activation(b_hi[:, o * HALF:(o + 1) * HALF], w_in[:rank, o], ACT.Identity)\
                       .then_inc(b_hi_ready, 1)

            def weight_hi(batch, par, k, o):
                act.wait_ge(w_summed, unit(batch, k, o) + 1)
                act.activation(wall[:, par, 0, k, o * HALF:(o + 1) * HALF], w_in[:, o], ACT.Identity)\
                   .then_inc(w_hi_ready, 1)

            def evacuate(turn, j, h):
                t = BODY * turn + j
                act.wait_ge(mm_done, 2 * t + h + 1)
                act.wait_ge(stored[j % 2], 16 * (TPB * turn + j // 2))
                act.activation(row[:, j % 2, h * HALF:(h + 1) * HALF], ps_out[h][:], ACT.Identity)\
                   .then_inc(evacuated[h], 1)

            def normalise(t, j):
                s = j % 2
                act.wait_ge(shift_ready, t + 1)
                act.activation(row[:, s], row[:, s], ACT.Identity, bias=shift[:, s:s + 1],
                               scale=rstd[:, s:s + 1]).then_inc(normed, 1)
                act.wait_ge(normed, t + 1)
                act.dma_start(io["out"][t], row[:, s]).then_inc(stored[s], 16)

            def split_y(t, j):
                act.wait_ge(y_turned, t + 1)
                act.activation(y_hi[:, :, (j % 2) * P:(j % 2 + 1) * P],
                               ps_y[:].rearrange("p (k t) -> p k t", k=KC), ACT.Identity)\
                   .then_inc(y_hi_ready, 1)

            def evacuate_h(turn, j):
                q = (j - 3) // 2
                slot = q % 2
                pair = TPB * turn + q
                act.wait_ge(h_done, pair + 1)
                act.wait_ge(h_stored[slot], 16 * (TPB // 2 * turn + q // 2 + 1))
                act.activation(h_out[:, slot], ps_h[:], ACT.Identity, bias=io["bin"][:]).then_inc(h_evacuated, 1)
                act.wait_ge(h_evacuated, pair + 2)
                act.dma_start(io["h"][:, bass.ds(2 * P * pair, 2 * P)] if not isinstance(pair, int)
                              else io["h"][:, 2 * P * pair:2 * P * (pair + 1)], h_out[:, slot])\
                   .then_inc(h_stored[slot], 16)

            split_x(0, 0)
            if low_rank:
                split_b(0)
                for k in range(KC):
                    split_a(0, k)
                    for o in range(2):
                        weight_hi(0, 0, k, o)

            def step(turn, j):
                t = BODY * turn + j
                guard, now = only_in(act, 0, j == BODY - 1, turn)
                with guard:
                    split_x(BODY * now + j + 1, j + 1)
                guard, now = only_in(act, 1, j == 0, turn)
                with guard:
                    normalise(BODY * now + j - 1, j + 1)

                def first(batch, par, k):
                    if k == 0:
                        split_b(batch)
                    split_a(batch, k)
                    weight_hi(batch, par, k, 0)
                weights_next(act, turn, j, first)
                if not low_rank:
                    evacuate(turn, j, 0)
                if project and j % 2:
                    guard, now = only_in(act, 1, j == 1, turn)
                    with guard:
                        evacuate_h(now, j)
                weights_next(act, turn, j, lambda batch, par, k: weight_hi(batch, par, k, 1))
                if project:
                    guard, now = only_in(act, 1, j == 0, turn)
                    with guard:
                        split_y(BODY * now + j - 1, j + 1)
                if not low_rank:
                    evacuate(turn, j, 1)

            steps(act, step)
            normalise(TILES - 1, 1)
            if project:
                split_y(TILES - 1, 1)
                evacuate_h(TILES // BODY, 1)
                for s in range(2):
                    act.wait_ge(h_stored[s], 16 * (TILES // 4 + 1))
            for s in range(2):
                act.wait_ge(stored[s], 16 * TILES // 2)

        @block.vector
        def _(dve):
            if project:
                nc.vector.memset(stats[:, 0, 0, 0:1], 0.0).then_inc(y_hi_ready, 1)
                nc.vector.memset(stats[:, 0, 0, 1:2], 0.0).then_inc(y_lo_ready, 1)
                nc.vector.memset(stats[:, 0, 0, 2:3], 0.0).then_inc(h_evacuated, 1)
                nc.vector.memset(stats[:, 0, 0, 3:4], 0.0).then_inc(h_stored[0], 16)
                nc.vector.memset(stats[:, 0, 0, 4:5], 0.0).then_inc(h_stored[1], 16)

            def split_x(t, j):
                dve.wait_ge(hi_ready, t + 1)
                src = ps_x if low_rank else x_in
                s = j % 2
                dve.tensor_tensor(x_lo[:, s].rearrange("p k t -> p (k t)"), src[:],
                                  x_hi[:, s].rearrange("p k t -> p (k t)").bitcast(F32), ALU.subtract)\
                   .then_inc(lo_ready, 1)

            def split_a(batch, k):
                dve.wait_ge(a_hi_ready, KC * batch + k + 1)
                dve.tensor_tensor(a_lo[:], a_in[:], a_hi[:].bitcast(F32), ALU.subtract).then_inc(a_lo_ready, 1)

            def scale_b(batch):
                for o in range(2):
                    dve.wait_ge(bt_loaded, 32 * (batch + 1))
                    coef = io["coef"][:, batch:batch + 1] if isinstance(batch, int)\
                        else io["coef"][:, bass.ds(batch, 1)]
                    dve.tensor_scalar(w_in[:rank, o], w_in[:rank, o], coef, None, ALU.mult).then_inc(bs_scaled, 1)
                for o in range(2):
                    dve.wait_ge(b_hi_ready, 2 * batch + o + 1)
                    dve.tensor_tensor(b_lo[:, o * HALF:(o + 1) * HALF], w_in[:rank, o],
                                      b_hi[:, o * HALF:(o + 1) * HALF].bitcast(F32), ALU.subtract)\
                       .then_inc(b_lo_ready, 1)

            def weight_sum(batch, k, o):
                n = unit(batch, k, o)
                dve.wait_ge(w_loaded[o], 16 * (KC * batch + k + 1))
                if o == k * P // HALF:
                    diag = w_in[:, o, k * P - o * HALF:(k + 1) * P - o * HALF]
                    dve.tensor_tensor(diag, diag, ident[:], ALU.add).then_inc(w_diag, 1)
                    dve.wait_ge(w_diag, KC * batch + k + 1)
                dve.wait_ge(w_product, n + 1)
                dve.tensor_tensor(w_in[:, o], ps_w[:], w_in[:, o], ALU.add).then_inc(w_summed, 1)

            def weight_lo(batch, par, k, o):
                dve.wait_ge(w_hi_ready, unit(batch, k, o) + 1)
                cols = slice(o * HALF, (o + 1) * HALF)
                dve.tensor_tensor(wall[:, par, 1, k, cols], w_in[:, o], wall[:, par, 0, k, cols].bitcast(F32),
                                  ALU.subtract).then_inc(w_lo_ready, 1)

            def half_stats(turn, j, h):
                t = BODY * turn + j
                s = j % 2
                cols = slice(h * HALF, (h + 1) * HALF)
                if low_rank:
                    dve.wait_ge(mm_done, 2 * t + h + 1)
                    dve.wait_ge(stored[s], 16 * (TPB * turn + j // 2))
                    dve.tensor_tensor(row[:, s, cols], ps_out[h][:], bias[:, cols], ALU.add)\
                       .then_inc(evacuated[h], 1)
                dve.wait_ge(evacuated[h], t + 1)
                dve.bn_stats(stats[:, s, h], row[:, s, cols]).then_inc(stats_ready, 1)

            def aggregate(t, j):
                s = j % 2
                due = dve.compute_val(2 * t + 2)
                dve.wait_ge(const_ready, 1)
                dve.wait_ge(stats_ready, due)
                dve.bn_aggr(mean_var[:, s], stats[:, s].rearrange("p a b -> p (a b)")).then_inc(mv_ready, 1)

            def split_y(t, j):
                dve.wait_ge(y_hi_ready, t + 2)
                cols = slice((j % 2) * P, (j % 2 + 1) * P)
                dve.tensor_tensor(y_lo[:, :, cols], ps_y[:].rearrange("p (k t) -> p k t", k=KC),
                                  y_hi[:, :, cols].bitcast(F32), ALU.subtract).then_inc(y_lo_ready, 1)

            split_x(0, 0)
            if low_rank:
                dve.wait_ge(bias_loaded, 16)
                scale_b(0)
                for k in range(KC):
                    split_a(0, k)
                    for o in range(2):
                        weight_sum(0, k, o)
                        weight_lo(0, 0, k, o)

            def step(turn, j):
                t = BODY * turn + j
                if j == 0:
                    guard, now = only_in(dve, 1, True, turn)
                    with guard:
                        half_stats(now - 1, BODY - 1, 1)
                        aggregate(BODY * now - 1, 1)
                else:
                    half_stats(turn, j - 1, 1)
                    aggregate(t - 1, j - 1)
                guard, now = only_in(dve, 0, j == BODY - 1, turn)
                with guard:
                    split_x(BODY * now + j + 1, j + 1)

                def first(batch, par, k):
                    if k == 0:
                        scale_b(batch)
                    split_a(batch, k)
                weights_next(dve, turn, j, first)
                half_stats(turn, j, 0)

                def second(batch, par, k):
                    for o in range(2):
                        weight_sum(batch, k, o)
                        weight_lo(batch, par, k, o)
                weights_next(dve, turn, j, second)
                if project:
                    guard, now = only_in(dve, 1, j == 0, turn)
                    with guard:
                        split_y(BODY * now + j - 1, j + 1)

            steps(dve, step)
            half_stats(TILES // BODY - 1, BODY - 1, 1)
            aggregate(TILES - 1, 1)
            if project:
                split_y(TILES - 1, 1)

        @block.gpsimd
        def _(pool):
            pool.memset(minus_half[:], -0.5).then_inc(const_ready, 1)
            pool.wait_ge(const_ready, 1)
            with pool.Fori(0, TILES // 2) as pair:
                for s in range(2):
                    t = 2 * pair + s
                    due = pool.compute_val(t + 1)
                    pool.wait_ge(const_ready, 1)
                    pool.wait_ge(mv_ready, due)
                    pool.tensor_scalar(var_eps[:, s:s + 1], mean_var[:, s, 1:2], EPS, 1.0, ALU.add, ALU.mult)\
                        .then_inc(ve_ready, 1)
                    pool.wait_ge(ve_ready, t + 1)
                    pool.tensor_tensor(rstd[:, s:s + 1], var_eps[:, s:s + 1], minus_half[:], ALU.pow)\
                        .then_inc(rstd_ready, 1)
                    pool.wait_ge(const_ready, 1)
                    pool.wait_ge(rstd_ready, due)
                    pool.tensor_scalar(shift[:, s:s + 1], mean_var[:, s, 0:1], rstd[:, s:s + 1], -1.0,
                                       ALU.mult, ALU.mult).then_inc(shift_ready, 1)


def setup_phase(nc, io, wall, ident, persist):
    with ExitStack() as ctx:
        def sb(name, shape, dt=F32):
            return ctx.enter_context(nc.sbuf_tensor(f"S_{name}", shape, dt))

        def sem(name):
            return ctx.enter_context(nc.semaphore(f"S_{name}"))

        NB = D // 32
        w_in = sb("w_in", [P, 2, D])
        m_in = sb("m_in", [P, 2, D], I32)
        block_sum = sb("block_sum", [P, 2, NB])
        block_on = sb("block_on", [P, 2, NB])
        same_block = sb("same_block", [P, P])
        centre = sb("centre", [P, P])
        win_in = sb("win_in", [P, KC, P])
        win_mean = sb("win_mean", [P, KC])
        bias_in = sb("bias_in", [P, LAYERS + 1])
        starts = sb("starts", [48, 4], I32)
        below = sb("below", [48, 4, 4])
        count = sb("count", [48, 4])
        adapter = sb("adapter", [48, 2])
        ps_block = [ctx.enter_context(nc.psum_tensor(f"S_ps_block{s}", [P, NB], F32)) for s in range(2)]
        ps_bias = ctx.enter_context(nc.psum_tensor("S_ps_bias", [P, LAYERS + 1], F32))

        consts = sem("consts")
        ident_ready = sem("ident_ready")
        w_loaded = [sem(f"w_loaded{s}") for s in range(2)]
        m_loaded = [sem(f"m_loaded{s}") for s in range(2)]
        small_loaded = sem("small_loaded")
        summed = sem("summed")
        spread = sem("spread")
        on_ready = sem("on_ready")
        masked = sem("masked")
        diag_ready = sem("diag_ready")
        hi_ready = sem("hi_ready")
        lo_ready = sem("lo_ready")
        dve_done = sem("dve_done")
        win_ready = sem("win_ready")
        win_hi_ready = sem("win_hi_ready")
        centre_ready = sem("centre_ready")
        bias_done = sem("bias_done")
        adapter_parts = sem("adapter_parts")

        block = ctx.enter_context(nc.Block())

        @block.sync
        def _(sp):
            for k in range(KC):
                s = k % 2
                if k >= 2:
                    sp.wait_ge(summed, k - 1)
                    sp.wait_ge(hi_ready, k - 1)
                    sp.wait_ge(lo_ready, k - 1)
                sp.dma_start(m_in[:, s], io["mask_t"][k]).then_inc(m_loaded[s], 16)
                sp.dma_start(w_in[:, s], io["w0_t"][k]).then_inc(w_loaded[s], 16)

        @block.scalar
        def _(act):
            act.dma_start(win_in[:], io["win_t"]).then_inc(small_loaded, 16)
            act.dma_start(bias_in[:], io["bias_stack"]).then_inc(small_loaded, 16)
            act.dma_start(starts[:], io["starts"].partition_broadcast(48)).then_inc(small_loaded, 16)
            for k in range(KC):
                s = k % 2
                act.wait_ge(diag_ready, k + 1)
                act.activation(wall[:, 1, 0, k], w_in[:, s], ACT.Identity).then_inc(hi_ready, 1)
            act.wait_ge(win_ready, 1)
            act.activation(persist["win_hi"][:].rearrange("p k d -> p (k d)"),
                           win_in[:].rearrange("p k d -> p (k d)"), ACT.Identity).then_inc(win_hi_ready, 1)

        @block.gpsimd
        def _(pool):
            pool.memset(ident[:], 0.0).then_inc(consts, 1)
            pool.memset(same_block[:], 0.0).then_inc(consts, 1)
            pool.memset(adapter[:], 1.0).then_inc(consts, 1)
            pool.wait_ge(consts, 3)
            for i in range(P // 32):
                pool.memset(same_block[32 * i:32 * i + 32, 32 * i:32 * i + 32], 1.0).then_inc(consts, 1)
            pool.wait_ge(consts, 3 + P // 32)
            pool.affine_select(out=ident[:], in_=ident[:], compare_op=ALU.not_equal, fill=1.0, base=0,
                               pattern=[[-1, P]], channel_multiplier=1).then_inc(ident_ready, 1)
            for i in range(2):
                pool.affine_select(out=adapter[:, i:i + 1], in_=adapter[:, i:i + 1], compare_op=ALU.is_ge,
                                   fill=0.0, base=-16 * (i + 1), pattern=[[0, 1]], channel_multiplier=1)\
                    .then_inc(adapter_parts, 1)
            for k in range(KC):
                s = k % 2
                pool.wait_ge(on_ready, k + 1)
                pool.wait_ge(w_loaded[s], 16 * (k // 2 + 1))
                w = w_in[:, s].rearrange("p (n c) -> p n c", n=NB)
                pool.tensor_tensor(w, w, block_on[:, s].unsqueeze(2).broadcast_to([P, NB, 32]), ALU.mult)\
                    .then_inc(masked, 1)

        @block.tensor
        def _(pe):
            pe.wait_ge(consts, 3 + P // 32)
            for k in range(KC):
                s = k % 2
                pe.wait_ge(summed, k + 1)
                if k >= 2:
                    pe.wait_ge(on_ready, k - 1)
                pe.matmul(ps_block[s][:], same_block[:], block_sum[:, s], start=True, stop=True).then_inc(spread, 1)
            pe.wait_ge(centre_ready, 1)
            pe.wait_ge(small_loaded, 48)
            pe.matmul(ps_bias[:], centre[:], bias_in[:], start=True, stop=True).then_inc(bias_done, 1)

        @block.vector
        def _(dve):
            def block_sums(k):
                s = k % 2
                dve.wait_ge(m_loaded[s], 16 * (k // 2 + 1))
                if k >= 2:
                    dve.wait_ge(spread, k - 1)
                dve.tensor_reduce(block_sum[:, s], m_in[:, s].rearrange("p (n c) -> p n c", n=NB), AX, ALU.add)\
                   .then_inc(summed, 1)

            def compare(k):
                s = k % 2
                dve.wait_ge(spread, k + 1)
                if k >= 2:
                    dve.wait_ge(masked, k - 1)
                dve.tensor_scalar(block_on[:, s], ps_block[s][:], 0.0, None, ALU.is_gt).then_inc(on_ready, 1)

            def finish(k):
                s = k % 2
                dve.wait_ge(ident_ready, 1)
                dve.wait_ge(masked, k + 1)
                diag = w_in[:, s, k * P:(k + 1) * P]
                dve.tensor_tensor(diag, diag, ident[:], ALU.add).then_inc(diag_ready, 1)
                dve.wait_ge(hi_ready, k + 1)
                dve.tensor_tensor(wall[:, 1, 1, k], w_in[:, s], wall[:, 1, 0, k].bitcast(F32), ALU.subtract)\
                   .then_inc(lo_ready, 1)

            block_sums(0)
            compare(0)
            for k in range(KC):
                if k + 1 < KC:
                    block_sums(k + 1)
                    compare(k + 1)
                finish(k)

            done = [0]

            def after(ins):
                done[0] += 1
                ins.then_inc(dve_done, 1)
                dve.wait_ge(dve_done, done[0])

            dve.wait_ge(small_loaded, 48)
            dve.wait_ge(adapter_parts, 2)
            after(dve.tensor_reduce(win_mean[:], win_in[:], AX, ALU.add))
            after(dve.tensor_scalar(win_mean[:], win_mean[:], 1.0 / P, None, ALU.mult))
            dve.tensor_tensor(win_in[:], win_in[:], win_mean[:].unsqueeze(2).broadcast_to([P, KC, P]), ALU.subtract)\
               .then_inc(win_ready, 1)
            dve.tensor_scalar(centre[:], ident[:], -1.0 / P, None, ALU.add).then_inc(centre_ready, 1)
            for b in range(BATCHES):
                after(dve.tensor_scalar(below[:, b], starts[:], float(b), None, ALU.is_le))
            after(dve.tensor_reduce(count[:], below[:], AX, ALU.add))
            after(dve.tensor_tensor(adapter[:, 0:1], adapter[:, 0:1], adapter[:, 1:2], ALU.add))
            after(dve.tensor_scalar(adapter[:, 0:1], adapter[:, 0:1], 2.0, None, ALU.add))
            after(dve.memset(persist["coef"][:48, BATCHES:BATCHES + 1], 0.0))
            after(dve.tensor_scalar(persist["coef"][:48, 0:BATCHES], count[:], adapter[:, 0:1], None, ALU.is_equal))
            dve.wait_ge(bias_done, 1)
            after(dve.tensor_copy(persist["bias_c"][:], ps_bias[:]))
            dve.wait_ge(win_hi_ready, 1)
            after(dve.tensor_tensor(persist["win_lo"][:], win_in[:], persist["win_hi"][:].bitcast(F32), ALU.subtract))


VECS = ["phz_re", "phz_im", "lc_re", "lc_im", "sc_lin", "ln1_w", "ln1_b", "ln2_w", "ln2_b"]
LEVELS = 10


def prepare_phase(nc, io, ident, m):
    with ExitStack() as ctx:
        def sb(name, shape, dt=F32):
            return ctx.enter_context(nc.sbuf_tensor(f"T_{name}", shape, dt))

        def sem(name):
            return ctx.enter_context(nc.semaphore(f"T_{name}"))

        vec = m["vec"]

        def v(name):
            return vec[:, VECS.index(name)]

        w2_mean = sb("w2_mean", [P, LAYERS * FCH])
        lnl = sb("lnl", [P, 2])
        bout = sb("bout", [1, D])
        brow = sb("brow", [1, D])
        ones = sb("ones", [1, P])
        centre = sb("centre", [P, P])
        sq_re = sb("sq_re", [P, LAYERS])
        sq_im = sb("sq_im", [P, LAYERS])
        r2 = sb("r2", [P, LAYERS])
        r2_safe = sb("r2_safe", [P, LAYERS])
        is_zero = sb("is_zero", [P, LAYERS])
        r_inv = sb("r_inv", [P, LAYERS])
        minus_half = sb("minus_half", [P, LAYERS])
        radius = sb("radius", [P, LAYERS])
        fix = sb("fix", [P, LAYERS])
        anchor = sb("anchor", [P, LEVELS, 2, LAYERS])
        cross = sb("cross", [P, 2, LAYERS, SEQ // 2])
        ps_b1 = ctx.enter_context(nc.psum_tensor("T_ps_b1", [P, LAYERS * FCH], F32))
        ps_row = [ctx.enter_context(nc.psum_tensor(f"T_ps_row{h}", [1, HALF], F32)) for h in range(2)]

        loaded = sem("loaded")
        row_loaded = sem("row_loaded")
        const_ready = sem("const_ready")
        r2_ready = sem("r2_ready")
        r_inv_ready = sem("r_inv_ready")
        radius_ready = sem("radius_ready")
        b1_product = sem("b1_product")
        row_product = sem("row_product")
        dve_done = sem("dve_done")
        wout_ready = sem("wout_ready")
        wout_hi_ready = sem("wout_hi_ready")
        row_ready = sem("row_ready")
        row_hi_ready = sem("row_hi_ready")

        block = ctx.enter_context(nc.Block())

        @block.sync
        def _(sp):
            sp.dma_start(vec[:], io["vec"]).then_inc(loaded, 16)
            sp.dma_start(m["w1"][:], io["mlp1_t"]).then_inc(loaded, 16)
            sp.dma_start(m["w2"][:], io["mlp2_t"]).then_inc(loaded, 16)
            sp.dma_start(m["b1"][:], io["mlp_b1"]).then_inc(loaded, 16)
            sp.dma_start(lnl[:], io["lnl"]).then_inc(loaded, 16)
            sp.dma_start(m["wout"][:], io["wout_t"]).then_inc(loaded, 16)
            sp.dma_start(bout[:], io["bout"]).then_inc(row_loaded, 16)

        @block.gpsimd
        def _(pool):
            pool.memset(minus_half[:], -0.5).then_inc(const_ready, 1)
            pool.wait_ge(const_ready, 1)
            pool.wait_ge(r2_ready, 1)
            pool.tensor_tensor(r_inv[:], r2_safe[:], minus_half[:], ALU.pow).then_inc(r_inv_ready, 1)

        @block.scalar
        def _(act):
            act.wait_ge(radius_ready, 1)
            act.activation(m["rho"][:], radius[:], ACT.Tanh)
            act.wait_ge(wout_ready, 1)
            act.activation(m["wout_hi"][:], m["wout"][:], ACT.Identity).then_inc(wout_hi_ready, 1)
            act.wait_ge(row_ready, 2)
            act.activation(m["row_hi"][:], brow[:], ACT.Identity).then_inc(row_hi_ready, 1)

        @block.tensor
        def _(pe):
            pe.wait_ge(loaded, 96)
            for n in range(LAYERS * FCH):
                l, q = n // FCH, n % FCH
                last = pe.matmul(ps_b1[:, n:n + 1], m["w1"][:, l, q * P:(q + 1) * P], v("ln2_b")[:, l:l + 1],
                                 start=True, stop=True)
            last.then_inc(b1_product, 1)
            for h in range(2):
                last = pe.matmul(ps_row[h][:], lnl[:, 1:2], m["wout"][:, h * HALF:(h + 1) * HALF],
                                 start=True, stop=True)
            last.then_inc(row_product, 1)

        @block.vector
        def _(dve):
            done = [0]

            def mark(ins):
                done[0] += 1
                ins.then_inc(dve_done, 1)

            def settle():
                dve.wait_ge(dve_done, done[0])

            def after(ins):
                mark(ins)
                settle()

            dve.wait_ge(loaded, 96)
            mark(dve.tensor_tensor(sq_re[:], v("phz_re"), v("phz_re"), ALU.mult))
            after(dve.tensor_tensor(sq_im[:], v("phz_im"), v("phz_im"), ALU.mult))
            after(dve.tensor_tensor(r2[:], sq_re[:], sq_im[:], ALU.add))
            dve.tensor_scalar(r2_safe[:], r2[:], 1e-37, None, ALU.max).then_inc(r2_ready, 1)
            after(dve.tensor_scalar(is_zero[:], r2[:], 1e-30, None, ALU.is_le))
            after(dve.tensor_scalar(fix[:], is_zero[:], -1.0, 1.0, ALU.mult, ALU.add))
            dve.wait_ge(r_inv_ready, 1)
            dve.tensor_tensor(radius[:], r2[:], r_inv[:], ALU.mult).then_inc(radius_ready, 1)
            dve.wait_ge(radius_ready, 1)
            after(dve.tensor_tensor(r_inv[:], r_inv[:], fix[:], ALU.mult))
            after(dve.tensor_tensor(sq_re[:], v("phz_re"), r_inv[:], ALU.mult))
            mark(dve.tensor_tensor(anchor[:, 0, 0], sq_re[:], is_zero[:], ALU.add))
            after(dve.scalar_tensor_tensor(anchor[:, 0, 1], v("phz_im"), -1.0, r_inv[:], ALU.mult, ALU.mult))
            for level in range(LEVELS):
                c, s = anchor[:, level, 0], anchor[:, level, 1]
                if level:
                    pc, ps = anchor[:, level - 1, 0], anchor[:, level - 1, 1]
                    mark(dve.tensor_tensor(sq_re[:], pc, pc, ALU.mult))
                    mark(dve.tensor_tensor(sq_im[:], ps, ps, ALU.mult))
                    after(dve.scalar_tensor_tensor(s, pc, 2.0, ps, ALU.mult, ALU.mult))
                    after(dve.tensor_tensor(c, sq_re[:], sq_im[:], ALU.subtract))
                mark(dve.tensor_tensor(sq_re[:], c, c, ALU.mult))
                after(dve.tensor_tensor(sq_im[:], s, s, ALU.mult))
                after(dve.tensor_tensor(fix[:], sq_re[:], sq_im[:], ALU.add))
                after(dve.tensor_scalar(fix[:], fix[:], -0.5, 1.5, ALU.mult, ALU.add))
                mark(dve.tensor_tensor(c, c, fix[:], ALU.mult))
                after(dve.tensor_tensor(s, s, fix[:], ALU.mult))
            table = m["table"]
            for i in range(2):
                mark(dve.tensor_copy(table[:, i, :, 0:1], anchor[:, 0, i].unsqueeze(2)))
            settle()
            for level in range(LEVELS):
                n = 2 ** level
                for l in range(LAYERS):
                    ac, an = anchor[:, level, 0, l:l + 1], anchor[:, level, 1, l:l + 1]
                    mark(dve.tensor_scalar(cross[:, 0, l, 0:n], table[:, 1, l, 0:n], an, None, ALU.mult))
                    mark(dve.tensor_scalar(cross[:, 1, l, 0:n], table[:, 1, l, 0:n], ac, None, ALU.mult))
                settle()
                for l in range(LAYERS):
                    ac, an = anchor[:, level, 0, l:l + 1], anchor[:, level, 1, l:l + 1]
                    mark(dve.scalar_tensor_tensor(table[:, 0, l, n:2 * n], table[:, 0, l, 0:n], ac,
                                                  cross[:, 0, l, 0:n], ALU.mult, ALU.subtract))
                    mark(dve.scalar_tensor_tensor(table[:, 1, l, n:2 * n], table[:, 0, l, 0:n], an,
                                                  cross[:, 1, l, 0:n], ALU.mult, ALU.add))
                settle()
            dve.wait_ge(b1_product, 1)
            mark(dve.tensor_tensor(m["b1"][:].rearrange("p l q -> p (l q)"), ps_b1[:],
                                   m["b1"][:].rearrange("p l q -> p (l q)"), ALU.add))
            for l in range(LAYERS):
                mark(dve.tensor_scalar(m["w1"][:, l], m["w1"][:, l], v("ln2_w")[:, l:l + 1], None, ALU.mult))
            w2 = m["w2"][:].rearrange("p l q d -> p (l q) d")
            after(dve.tensor_reduce(w2_mean[:], w2, AX, ALU.add))
            after(dve.tensor_scalar(w2_mean[:], w2_mean[:], 1.0 / P, None, ALU.mult))
            mark(dve.tensor_tensor(w2, w2, w2_mean[:].unsqueeze(2).broadcast_to([P, LAYERS * FCH, P]), ALU.subtract))
            after(dve.tensor_scalar(centre[:], ident[:], -1.0 / P, None, ALU.add))
            for l in range(LAYERS):
                mark(dve.tensor_scalar(m["mix"][:, l], centre[:], v("sc_lin")[:, l:l + 1], None, ALU.mult))
            dve.wait_ge(row_product, 1)
            dve.wait_ge(row_loaded, 16)
            dve.tensor_scalar(m["wout"][:], m["wout"][:], lnl[:, 0:1], None, ALU.mult).then_inc(wout_ready, 1)
            for h in range(2):
                cols = slice(h * HALF, (h + 1) * HALF)
                dve.tensor_tensor(brow[:, cols], ps_row[h][:], bout[:, cols], ALU.add).then_inc(row_ready, 1)
            after(dve.memset(ones[:], 1.0))
            mark(dve.tensor_copy(m["ones"][:], ones[:]))
            dve.wait_ge(wout_hi_ready, 1)
            mark(dve.tensor_tensor(m["wout_lo"][:], m["wout"][:], m["wout_hi"][:].bitcast(F32), ALU.subtract))
            dve.wait_ge(row_hi_ready, 1)
            mark(dve.tensor_tensor(m["row_lo"][:], brow[:], m["row_hi"][:].bitcast(F32), ALU.subtract))


def column_variance(pe, out, squares, mean_col):
    for c in range(HALF // P):
        last = pe.matmul(out[:, c:c + 1], squares[:, c * P:(c + 1) * P], mean_col[:], start=True, stop=True)
    return last


def spread_rows(pe, out, cols, ident):
    for c in range(HALF // P):
        last = pe.transpose(out[:, c * P:(c + 1) * P], cols[:, c:c + 1].broadcast_to([P, P]), ident[:])
    return last


def small_model_phase(nc, io, ident, m):
    with ExitStack() as ctx:
        def sb(name, shape, dt=F32):
            return ctx.enter_context(nc.sbuf_tensor(f"M_{name}", shape, dt))

        def psum(name):
            return ctx.enter_context(nc.psum_tensor(f"M_{name}", [P, HALF], F32))

        def sem(name):
            return ctx.enter_context(nc.semaphore(f"M_{name}"))

        vec, table, h = m["vec"], m["table"], m["h"]
        mean_col = sb("mean_col", [P, 1])
        minus_half = sb("minus_half", [P, 4])
        squares1 = sb("squares1", [P, HALF])
        squares2 = sb("squares2", [P, HALF])
        start = sb("start", [P, 1])
        var1 = sb("var1", [P, 4])
        var2 = sb("var2", [P, 4])
        rstd1 = sb("rstd1", [P, 4])
        rstd2 = sb("rstd2", [P, 4])
        z1 = sb("z1", [P, HALF])
        x = sb("x", [P, HALF])
        x_cos = sb("x_cos", [P, HALF])
        x_sin = sb("x_sin", [P, HALF])
        u = sb("u", [P, 2, 2, HALF])
        y_cos = sb("y_cos", [P, HALF])
        y_sin = sb("y_sin", [P, HALF])
        y = sb("y", [P, 2, HALF])
        y_hi = sb("y_hi", [P, HALF], F32R)
        y_lo = sb("y_lo", [P, HALF], F32R)
        z2 = sb("z2", [P, HALF])
        z2_hi = sb("z2_hi", [P, 2, HALF], F32R)
        z2_lo = sb("z2_lo", [P, 2, HALF], F32R)
        g = sb("g", [P, 2, HALF])
        g_hi = sb("g_hi", [P, 2, HALF], F32R)
        g_lo = sb("g_lo", [P, 2, HALF], F32R)
        mix_hi = sb("mix_hi", [P, P], F32R)
        mix_lo = sb("mix_lo", [P, P], F32R)
        w1_hi = sb("w1_hi", [P, FCH * P], F32R)
        w1_lo = sb("w1_lo", [P, FCH * P], F32R)
        w2_hi = sb("w2_hi", [P, FCH * P], F32R)
        w2_lo = sb("w2_lo", [P, FCH * P], F32R)
        ps_r1, ps_r2, ps_mix, ps_o = psum("ps_r1"), psum("ps_r2"), psum("ps_mix"), psum("ps_o")
        ps_f = [psum(f"ps_f{i}") for i in range(2)]

        h_loaded = sem("h_loaded")
        consts = sem("consts")
        h_ready = sem("h_ready")
        h_mid = sem("h_mid")
        sq1_ready, sq2_ready = sem("sq1_ready"), sem("sq2_ready")
        v1_done, v2_done = sem("v1_done"), sem("v2_done")
        var1_ready, var2_ready = sem("var1_ready"), sem("var2_ready")
        rstd1_ready, rstd2_ready = sem("rstd1_ready"), sem("rstd2_ready")
        spread1, spread2 = sem("spread1"), sem("spread2")
        z1_ready, z2_ready = sem("z1_ready"), sem("z2_ready")
        x_ready = sem("x_ready")
        x_cos_ready, x_sin_ready = sem("x_cos_ready"), sem("x_sin_ready")
        u_ready = sem("u_ready")
        y_cos_ready, y_sin_ready = sem("y_cos_ready"), sem("y_sin_ready")
        y_ready, y_hi_ready, y_lo_ready = sem("y_ready"), sem("y_hi_ready"), sem("y_lo_ready")
        mixed = sem("mixed")
        z2_hi_ready, z2_lo_ready = sem("z2_hi_ready"), sem("z2_lo_ready")
        f_done = sem("f_done")
        g_ready, g_hi_ready, g_lo_ready = sem("g_ready"), sem("g_hi_ready"), sem("g_lo_ready")
        o_done = sem("o_done")
        mix_hi_ready, mix_lo_ready = sem("mix_hi_ready"), sem("mix_lo_ready")
        w_hi_ready, w_lo_ready = sem("w_hi_ready"), sem("w_lo_ready")

        def of_layer(ap, layer):
            return ap[:, layer:layer + 1] if isinstance(layer, int) else ap[:, bass.ds(layer, 1)]

        def tokens(place):
            return slice(place * HALF, (place + 1) * HALF)

        def run(eng, stages):
            def step(turn, at):
                for stage, part in stages:
                    lag = "ABCD".index(stage)
                    if at < lag:
                        continue
                    over = at - lag >= UNITS
                    with (eng.If(turn < LAYERS - 1) if over else nullcontext()):
                        layer = (turn + 1) % LAYERS if over else turn
                        part(UNITS * turn + at - lag, layer, (at - lag) % UNITS)
            for at in range(3):
                step(0, at)
            with eng.Fori(0, LAYERS) as turn:
                for at in range(3, UNITS + 3):
                    step(turn, at)

        block = ctx.enter_context(nc.Block())

        @block.sync
        def _(sp):
            sp.dma_start(h[:], io["h"]).then_inc(h_loaded, 16)

        @block.tensor
        def _(pe):
            def mix(n, layer, place):
                pe.wait_ge(y_hi_ready, n + 1)
                pe.wait_ge(y_lo_ready, n + 1)
                if place == 0:
                    pe.wait_ge(mix_hi_ready, n + UNITS)
                    pe.wait_ge(mix_lo_ready, n + UNITS)
                pe.matmul(ps_mix[:], mix_hi[:], y_hi[:], start=True, stop=False)
                pe.matmul(ps_mix[:], mix_hi[:], y_lo[:], start=False, stop=False)
                pe.matmul(ps_mix[:], mix_lo[:], y_hi[:], start=False, stop=True).then_inc(mixed, 1)

            def hidden(q):
                def part(n, layer, place):
                    if q == 0:
                        pe.wait_ge(z2_hi_ready, n + 1)
                        pe.wait_ge(z2_lo_ready, n + 1)
                        if place == 0:
                            pe.wait_ge(w_hi_ready, 2 * n + 2 * UNITS)
                            pe.wait_ge(w_lo_ready, 2 * n + 2 * UNITS)
                    if q >= 2:
                        pe.wait_ge(g_ready, FCH * n + q - 1)
                    s = place % 2
                    cols = slice(q * P, (q + 1) * P)
                    bank = ps_f[q % 2]
                    pe.matmul(bank[:], w1_hi[:, cols], z2_hi[:, s], start=True, stop=False)
                    pe.matmul(bank[:], w1_hi[:, cols], z2_lo[:, s], start=False, stop=False)
                    pe.matmul(bank[:], w1_lo[:, cols], z2_hi[:, s], start=False, stop=True).then_inc(f_done, 1)
                return part

            def back(q):
                def part(n, layer, place):
                    pe.wait_ge(g_hi_ready, FCH * n + q + 1)
                    pe.wait_ge(g_lo_ready, FCH * n + q + 1)
                    if q == 0:
                        pe.wait_ge(h_ready, n + UNITS)
                    s = q % 2
                    cols = slice(q * P, (q + 1) * P)
                    pe.matmul(ps_o[:], w2_hi[:, cols], g_hi[:, s], start=(q == 0), stop=False)
                    pe.matmul(ps_o[:], w2_hi[:, cols], g_lo[:, s], start=False, stop=False)
                    last = pe.matmul(ps_o[:], w2_lo[:, cols], g_hi[:, s], start=False, stop=(q == FCH - 1))
                    if q == FCH - 1:
                        last.then_inc(o_done, 1)
                return part

            def variance1(n, layer, place):
                pe.wait_ge(sq1_ready, n + 1)
                column_variance(pe, ps_r1, squares1, mean_col).then_inc(v1_done, 1)

            def variance2(n, layer, place):
                pe.wait_ge(sq2_ready, n + 1)
                column_variance(pe, ps_r2, squares2, mean_col).then_inc(v2_done, 1)

            def spread_rstd1(n, layer, place):
                pe.wait_ge(rstd1_ready, n + 1)
                spread_rows(pe, ps_r1, rstd1, ident).then_inc(spread1, 1)

            def spread_rstd2(n, layer, place):
                pe.wait_ge(rstd2_ready, n + 1)
                spread_rows(pe, ps_r2, rstd2, ident).then_inc(spread2, 1)

            pe.wait_ge(consts, 2)
            run(pe, [("C", mix), ("D", hidden(0)), ("D", hidden(1)), ("A", variance1), ("C", variance2),
                     ("D", back(0)), ("D", hidden(2)), ("A", spread_rstd1), ("D", back(1)), ("D", hidden(3)),
                     ("C", spread_rstd2), ("D", back(2)), ("D", back(3))])

        @block.scalar
        def _(act):
            def split_y(n, layer, place):
                if place == 0:
                    src = m["mix"][:, layer] if isinstance(layer, int) else \
                        m["mix"][:, bass.ds(layer, 1)].rearrange("p a d -> p (a d)")
                    if not (isinstance(n, int) and n == 0):
                        act.wait_ge(mixed, n)
                    act.activation(mix_hi[:], src, ACT.Identity).then_inc(mix_hi_ready, UNITS)
                act.wait_ge(y_ready, n + 1)
                act.activation(y_hi[:], y[:, place % 2], ACT.Identity).then_inc(y_hi_ready, 1)

            def square1(n, layer, place):
                act.wait_ge(h_ready, n + 1)
                act.activation(squares1[:], h[:, tokens(place)], ACT.Square).then_inc(sq1_ready, 1)

            def square2(n, layer, place):
                act.wait_ge(h_mid, n + 1)
                act.activation(squares2[:], h[:, tokens(place)], ACT.Square).then_inc(sq2_ready, 1)

            def split_weights(n, layer, place):
                if place == 0:
                    act.wait_ge(o_done, n)
                    for w, w_hi in ((m["w1"], w1_hi), (m["w2_flat"], w2_hi)):
                        src = w[:, layer] if isinstance(layer, int) else \
                            w[:, bass.ds(layer, 1)].rearrange("p a d -> p (a d)")
                        act.activation(w_hi[:], src, ACT.Identity).then_inc(w_hi_ready, UNITS)

            def silu_hidden(q):
                def part(n, layer, place):
                    due = act.compute_val(FCH * n + q + 1)
                    act.wait_ge(consts, 2)
                    act.wait_ge(f_done, due)
                    b1 = m["b1"][:, :, q]
                    act.activation(g[:, q % 2], ps_f[q % 2][:], ACT.Silu, bias=of_layer(b1, layer))\
                       .then_inc(g_ready, 1)
                return part

            def split_g(q):
                def part(n, layer, place):
                    act.wait_ge(g_ready, FCH * n + q + 1)
                    act.activation(g_hi[:, q % 2], g[:, q % 2], ACT.Identity).then_inc(g_hi_ready, 1)
                return part

            def silu_x(n, layer, place):
                due = act.compute_val(n + 1)
                act.wait_ge(consts, 2)
                act.wait_ge(z1_ready, due)
                act.activation(x[:], z1[:], ACT.Silu, bias=of_layer(vec[:, VECS.index("ln1_b")], layer),
                               scale=of_layer(vec[:, VECS.index("ln1_w")], layer)).then_inc(x_ready, 1)

            def split_z2(n, layer, place):
                act.wait_ge(z2_ready, n + 1)
                act.activation(z2_hi[:, place % 2], z2[:], ACT.Identity).then_inc(z2_hi_ready, 1)

            run(act, [("D", split_weights), ("C", split_y), ("A", square1), ("D", silu_hidden(0)), ("C", square2), ("D", split_g(0)),
                      ("D", silu_hidden(1)), ("D", split_g(1)), ("D", silu_hidden(2)), ("D", split_g(2)),
                      ("A", silu_x), ("D", silu_hidden(3)), ("D", split_g(3)), ("C", split_z2)])

        @block.vector
        def _(dve):
            dve.memset(mean_col[:], 1.0 / P).then_inc(consts, 1)
            dve.wait_ge(h_loaded, 16)
            dve.memset(start[:], 0.0).then_inc(h_ready, UNITS)

            def split_y(n, layer, place):
                if place == 0:
                    src = m["mix"][:, layer] if isinstance(layer, int) else \
                        m["mix"][:, bass.ds(layer, 1)].rearrange("p a d -> p (a d)")
                    dve.wait_ge(mix_hi_ready, n + UNITS)
                    dve.tensor_tensor(mix_lo[:], src, mix_hi[:].bitcast(F32), ALU.subtract)\
                       .then_inc(mix_lo_ready, UNITS)
                dve.wait_ge(y_hi_ready, n + 1)
                dve.tensor_tensor(y_lo[:], y[:, place % 2], y_hi[:].bitcast(F32), ALU.subtract)\
                   .then_inc(y_lo_ready, 1)

            def add_mixed(n, layer, place):
                dve.wait_ge(mixed, n + 1)
                dve.wait_ge(h_ready, n + 1)
                dve.tensor_tensor(h[:, tokens(place)], ps_mix[:], h[:, tokens(place)], ALU.add).then_inc(h_mid, 1)

            def take_var1(n, layer, place):
                dve.wait_ge(v1_done, n + 1)
                dve.tensor_scalar(var1[:], ps_r1[:, 0:4], EPS, None, ALU.add).then_inc(var1_ready, 1)

            def take_var2(n, layer, place):
                dve.wait_ge(v2_done, n + 1)
                dve.tensor_scalar(var2[:], ps_r2[:, 0:4], EPS, None, ALU.add).then_inc(var2_ready, 1)

            def scan(i):
                def part(n, layer, place):
                    s = place % 2
                    dve.wait_ge((x_cos_ready, x_sin_ready)[i], n + 1)
                    dve.wait_ge(u_ready, 2 * n)
                    first = of_layer(vec[:, VECS.index(("lc_re", "lc_im")[i])], layer) if s == 0 else \
                        u[:, 0, i, HALF - 1:HALF]
                    dve.tensor_tensor_scan(u[:, s, i], of_layer(m["rho"], layer).broadcast_to([P, HALF]),
                                           (x_cos, x_sin)[i][:], first, ALU.mult, ALU.add).then_inc(u_ready, 1)
                return part

            def rotate_back(n, layer, place):
                s = place % 2
                dve.wait_ge(u_ready, 2 * n + 1)
                dve.tensor_tensor(y_cos[:], u[:, s, 0], rotation(m, 0, layer, s), ALU.mult).then_inc(y_cos_ready, 1)

            def scale1(n, layer, place):
                dve.wait_ge(spread1, n + 1)
                dve.tensor_tensor(z1[:], ps_r1[:], h[:, tokens(place)], ALU.mult).then_inc(z1_ready, 1)

            def scale2(n, layer, place):
                dve.wait_ge(spread2, n + 1)
                dve.wait_ge(h_mid, n + 1)
                dve.tensor_tensor(z2[:], ps_r2[:], h[:, tokens(place)], ALU.mult).then_inc(z2_ready, 1)

            def split_weights(n, layer, place):
                if place == 0:
                    for i, (w, w_hi, w_lo) in enumerate(((m["w1"], w1_hi, w1_lo), (m["w2_flat"], w2_hi, w2_lo))):
                        src = w[:, layer] if isinstance(layer, int) else \
                            w[:, bass.ds(layer, 1)].rearrange("p a d -> p (a d)")
                        dve.wait_ge(w_hi_ready, 2 * n + UNITS * (i + 1))
                        dve.tensor_tensor(w_lo[:], src, w_hi[:].bitcast(F32), ALU.subtract)\
                           .then_inc(w_lo_ready, UNITS)

            def split_g(q):
                def part(n, layer, place):
                    dve.wait_ge(g_hi_ready, FCH * n + q + 1)
                    dve.tensor_tensor(g_lo[:, q % 2], g[:, q % 2], g_hi[:, q % 2].bitcast(F32), ALU.subtract)\
                       .then_inc(g_lo_ready, 1)
                return part

            def split_z2(n, layer, place):
                s = place % 2
                dve.wait_ge(z2_hi_ready, n + 1)
                dve.tensor_tensor(z2_lo[:, s], z2[:], z2_hi[:, s].bitcast(F32), ALU.subtract)\
                   .then_inc(z2_lo_ready, 1)

            def add_hidden(n, layer, place):
                dve.wait_ge(o_done, n + 1)
                dve.wait_ge(h_mid, n + 1)
                dve.scalar_tensor_tensor(h[:, tokens(place)], ps_o[:], of_layer(m["b2"], layer),
                                         h[:, tokens(place)], ALU.add, ALU.add).then_inc(h_ready, 1)

            run(dve, [("D", split_weights), ("C", split_y), ("C", add_mixed), ("A", take_var1), ("D", split_g(0)), ("B", scan(0)),
                      ("C", take_var2), ("D", split_g(1)), ("B", scan(1)), ("A", scale1), ("D", split_g(2)),
                      ("B", rotate_back), ("C", scale2), ("D", split_g(3)), ("C", split_z2), ("D", add_hidden)])

        @block.gpsimd
        def _(pool):
            pool.memset(minus_half[:], -0.5).then_inc(consts, 1)
            pool.wait_ge(consts, 2)

            def rotate(i):
                def part(n, layer, place):
                    if i == 0:
                        due, free = pool.compute_val(n + 1), pool.compute_val(2 * n)
                        pool.wait_ge(consts, 2)
                        pool.wait_ge(x_ready, due)
                        pool.wait_ge(u_ready, free)
                    pool.tensor_tensor((x_cos, x_sin)[i][:], x[:], rotation(m, i, layer, place % 2), ALU.mult)\
                        .then_inc((x_cos_ready, x_sin_ready)[i], 1)
                return part

            def root1(n, layer, place):
                pool.wait_ge(var1_ready, n + 1)
                pool.tensor_tensor(rstd1[:], var1[:], minus_half[:], ALU.pow).then_inc(rstd1_ready, 1)

            def root2(n, layer, place):
                pool.wait_ge(var2_ready, n + 1)
                pool.tensor_tensor(rstd2[:], var2[:], minus_half[:], ALU.pow).then_inc(rstd2_ready, 1)

            def rotate_back(n, layer, place):
                s = place % 2
                due = pool.compute_val(2 * n + 2)
                pool.wait_ge(consts, 2)
                pool.wait_ge(u_ready, due)
                pool.tensor_tensor(y_sin[:], u[:, s, 1], rotation(m, 1, layer, s), ALU.mult)\
                    .then_inc(y_sin_ready, 1)

            def real_part(n, layer, place):
                pool.wait_ge(y_cos_ready, n + 1)
                pool.wait_ge(y_sin_ready, n + 1)
                pool.tensor_tensor(y[:, place % 2], y_cos[:], y_sin[:], ALU.add).then_inc(y_ready, 1)

            run(pool, [("B", rotate(0)), ("B", rotate(1)), ("A", root1), ("C", root2), ("B", rotate_back),
                       ("B", real_part)])


def rotation(m, i, layer, half):
    cols = slice(half * HALF, (half + 1) * HALF)
    if isinstance(layer, int):
        return m["table"][:, i, layer, cols]
    return m["table"][:, i, bass.ds(layer, 1), cols].rearrange("p a t -> p (a t)")

def readout_phase(nc, io, ident, m, q):
    TPU = HALF // P
    with ExitStack() as ctx:
        def sb(name, shape, dt=F32):
            return ctx.enter_context(nc.sbuf_tensor(f"C_{name}", shape, dt))

        def psum(name, shape):
            return ctx.enter_context(nc.psum_tensor(f"C_{name}", shape, F32))

        def sem(name):
            return ctx.enter_context(nc.semaphore(f"C_{name}"))

        h = m["h"]
        mean_col = sb("mean_col", [P, 1])
        minus_half = sb("minus_half", [P, TPU])
        token_weight = sb("token_weight", [P, 1])
        routed = sb("routed", [P, 2])
        start = sb("start", [P, 1])
        squares = sb("squares", [P, HALF])
        var = sb("var", [P, TPU])
        z_rstd = sb("z_rstd", [P, TPU])
        z = sb("z", [P, HALF])
        z_hi = sb("z_hi", [P, 2, HALF], F32R)
        z_lo = sb("z_lo", [P, 2, HALF], F32R)
        x_in = sb("x_in", [P, 2, D])
        row = sb("row", [P, 2, D])
        stats = sb("stats", [P, 2, 2, 6])
        mean_var = sb("mean_var", [P, 2, 2])
        var_eps = sb("var_eps", [P, 2])
        rstd = sb("rstd", [P, 2])
        shift = sb("shift", [P, 2])
        total = sb("total", [P, D])
        ps_out = [[psum(f"ps_out{s}{i}", [P, HALF]) for i in range(2)] for s in range(2)]
        ps_var = psum("ps_var", [P, TPU])
        ps_z = psum("ps_z", [P, HALF])
        ps_q = psum("ps_q", [P, KC])

        consts = sem("consts")
        squared = sem("squared")
        var_done = sem("var_done")
        var_ready = sem("var_ready")
        z_rstd_ready = sem("z_rstd_ready")
        spread = sem("spread")
        z_ready, z_hi_ready, z_lo_ready = sem("z_ready"), sem("z_hi_ready"), sem("z_lo_ready")
        x_loaded = [sem(f"x_loaded{s}") for s in range(2)]
        mm_done = sem("mm_done")
        added = sem("added")
        stats_ready, mv_ready, ve_ready = sem("stats_ready"), sem("mv_ready"), sem("ve_ready")
        rstd_ready, shift_ready = sem("rstd_ready"), sem("shift_ready")
        normed = sem("normed")
        stored = [sem(f"stored{s}") for s in range(2)]
        totalled = sem("totalled")
        q_done = sem("q_done")
        q_taken = sem("q_taken")

        def steps(eng, step):
            with eng.Fori(0, BATCHES) as batch:
                for j in range(TPB):
                    step(batch, j)

        def before(batch):
            return (batch + (BATCHES - 1)) % BATCHES

        def earlier(eng, batch, j, part):
            if j > 0:
                part(batch, j - 1)
            else:
                with eng.If(batch > 0):
                    part(before(batch), TPB - 1)

        def next_unit(eng, batch, j, part):
            with (eng.If(batch < BATCHES - 1) if j >= TPU else nullcontext()):
                part(2 * batch + j // TPU + 1, (j // TPU + 1) % 2)

        block = ctx.enter_context(nc.Block())

        @block.sync
        def _(sp):
            def step(batch, j):
                t = TPB * batch + j
                sp.wait_ge(added, 2 * t + 2)
                sp.dma_start(x_in[:, j % 2], io["x"][t]).then_inc(x_loaded[j % 2], 16)
            sp.wait_ge(consts, 4)
            steps(sp, step)

        @block.tensor
        def _(pe):
            def variance(n, slot):
                pe.wait_ge(squared, n + 1)
                column_variance(pe, ps_var, squares, mean_col).then_inc(var_done, 1)

            def spread_rstd(n, slot):
                pe.wait_ge(z_rstd_ready, n + 1)
                pe.wait_ge(z_ready, n)
                spread_rows(pe, ps_z, z_rstd, ident).then_inc(spread, 1)

            def product(t, j, i):
                pe.wait_ge(added, 2 * t + i + 1)
                slot, c = j // TPU, j % TPU
                hi, lo = z_hi[:, slot, c * P:(c + 1) * P], z_lo[:, slot, c * P:(c + 1) * P]
                cols = slice(i * HALF, (i + 1) * HALF)
                bank = ps_out[j % 2][i]
                pe.matmul(bank[:], hi, m["wout_hi"][:, cols], start=True, stop=False)
                pe.matmul(bank[:], hi, m["wout_lo"][:, cols], start=False, stop=False)
                pe.matmul(bank[:], lo, m["wout_hi"][:, cols], start=False, stop=False)
                pe.matmul(bank[:], m["ones"][:], m["row_hi"][:, cols], start=False, stop=False)
                pe.matmul(bank[:], m["ones"][:], m["row_lo"][:, cols], start=False, stop=True).then_inc(mm_done, 1)

            def reduce_total(batch):
                pe.wait_ge(totalled, (TPB - 1) * (batch + 1))
                for k in range(KC):
                    last = pe.matmul(ps_q[:, k:k + 1], total[:, k * P:(k + 1) * P], token_weight[:],
                                     start=True, stop=True)
                last.then_inc(q_done, 1)

            pe.wait_ge(consts, 4)
            variance(0, 0)
            spread_rstd(0, 0)

            def step(batch, j):
                t = TPB * batch + j
                if j % TPU == 0:
                    pe.wait_ge(z_hi_ready, 2 * batch + j // TPU + 1)
                    pe.wait_ge(z_lo_ready, 2 * batch + j // TPU + 1)
                product(t, j, 0)
                if j % TPU == 1:
                    next_unit(pe, batch, j, variance)
                if j % TPU == 3:
                    next_unit(pe, batch, j, spread_rstd)
                if j == 1:
                    with pe.If(batch > 0):
                        reduce_total(before(batch))
                product(t, j, 1)
            steps(pe, step)
            reduce_total(BATCHES - 1)

        @block.scalar
        def _(act):
            def square(n, slot):
                act.wait_ge(var_done, n)
                tokens = h[:, 0:HALF] if isinstance(n, int) else h[:, bass.ds(HALF * (n % UNITS), HALF)]
                act.activation(squares[:], tokens, ACT.Square).then_inc(squared, 1)

            def split_z(n, slot):
                if not isinstance(n, int):
                    act.wait_ge(mm_done, 2 * TPU * (n - 1))
                act.wait_ge(z_ready, n + 1)
                act.activation(z_hi[:, slot], z[:], ACT.Identity).then_inc(z_hi_ready, 1)

            def normalise(batch, j):
                s = j % 2
                act.wait_ge(shift_ready, TPB * batch + j + 1)
                act.activation(row[:, s], row[:, s], ACT.Identity, bias=shift[:, s:s + 1],
                               scale=rstd[:, s:s + 1]).then_inc(normed, 1)
                act.wait_ge(normed, TPB * batch + j + 1)
                act.dma_start(io["out"][TPB * batch + j], row[:, s]).then_inc(stored[s], 16)

            square(0, 0)
            split_z(0, 0)

            def step(batch, j):
                if j % TPU == 0:
                    next_unit(act, batch, j, square)
                earlier(act, batch, j, normalise)
                if j % TPU == 3:
                    next_unit(act, batch, j, split_z)
            steps(act, step)
            normalise(BATCHES - 1, TPB - 1)
            for s in range(2):
                act.wait_ge(stored[s], 16 * TILES // 2)

        @block.vector
        def _(dve):
            dve.memset(mean_col[:], 1.0 / P).then_inc(consts, 1)
            dve.memset(start[:], 0.0).then_inc(added, 4)

            def take_var(n, slot):
                dve.wait_ge(var_done, n + 1)
                dve.tensor_scalar(var[:], ps_var[:], EPS, None, ALU.add).then_inc(var_ready, 1)

            def scale(n, slot):
                dve.wait_ge(spread, n + 1)
                dve.wait_ge(z_hi_ready, n)
                tokens = h[:, 0:HALF] if isinstance(n, int) else h[:, bass.ds(HALF * (n % UNITS), HALF)]
                dve.tensor_tensor(z[:], ps_z[:], tokens, ALU.mult).then_inc(z_ready, 1)

            def split_z(n, slot):
                dve.wait_ge(z_hi_ready, n + 1)
                dve.tensor_tensor(z_lo[:, slot], z[:], z_hi[:, slot].bitcast(F32), ALU.subtract)\
                   .then_inc(z_lo_ready, 1)

            def half(batch, j, i):
                t = TPB * batch + j
                s = j % 2
                cols = slice(i * HALF, (i + 1) * HALF)
                if i == 0:
                    dve.wait_ge(x_loaded[s], 16 * (TPB // 2 * batch + j // 2 + 1))
                    dve.wait_ge(stored[s], 16 * (TPB // 2 * batch + j // 2))
                dve.wait_ge(mm_done, 2 * t + i + 1)
                dve.tensor_tensor(row[:, s, cols], ps_out[s][i][:], x_in[:, s, cols], ALU.add).then_inc(added, 1)
                dve.wait_ge(added, 2 * t + i + 5)
                dve.bn_stats(stats[:, s, i], row[:, s, cols]).then_inc(stats_ready, 1)

            def aggregate(batch, j):
                due = dve.compute_val(2 * (TPB * batch + j) + 2)
                dve.wait_ge(consts, 4)
                dve.wait_ge(stats_ready, due)
                dve.bn_aggr(mean_var[:, j % 2], stats[:, j % 2].rearrange("p a b -> p (a b)")).then_inc(mv_ready, 1)

            def add_up(batch, j):
                if j == 0:
                    return
                s = j % 2
                dve.wait_ge(normed, TPB * batch + j + 1)
                if j == 1:
                    dve.wait_ge(q_done, batch)
                    dve.tensor_scalar(total[:], row[:, s], routed[:, 0:1], None, ALU.mult).then_inc(totalled, 1)
                    return
                dve.wait_ge(totalled, (TPB - 1) * batch + j - 1)
                if j == TPB - 1:
                    dve.scalar_tensor_tensor(total[:], row[:, s], routed[:, 1:2], total[:], ALU.mult, ALU.add)\
                       .then_inc(totalled, 1)
                else:
                    dve.tensor_tensor(total[:], row[:, s], total[:], ALU.add).then_inc(totalled, 1)

            def take_q(batch):
                dve.wait_ge(q_done, batch + 1)
                column = q[:, :, batch:batch + 1] if isinstance(batch, int) else q[:, :, bass.ds(batch, 1)]
                dve.tensor_copy(column, ps_q[:].unsqueeze(2)).then_inc(q_taken, 1)

            take_var(0, 0)
            scale(0, 0)
            split_z(0, 0)

            def step(batch, j):
                earlier(dve, batch, j, aggregate)
                half(batch, j, 0)
                if j % TPU == 1:
                    next_unit(dve, batch, j, take_var)
                if j % TPU == 3:
                    next_unit(dve, batch, j, scale)
                earlier(dve, batch, j, add_up)
                half(batch, j, 1)
                if j % TPU == 3:
                    next_unit(dve, batch, j, split_z)
                if j == 1:
                    with dve.If(batch > 0):
                        take_q(before(batch))
            steps(dve, step)
            aggregate(BATCHES - 1, TPB - 1)
            add_up(BATCHES - 1, TPB - 1)
            take_q(BATCHES - 1)

        @block.gpsimd
        def _(pool):
            pool.memset(minus_half[:], -0.5).then_inc(consts, 1)
            pool.memset(token_weight[:], 1.0 / (ROUTED_END - ROUTED_START)).then_inc(consts, 1)
            pool.memset(routed[:], 1.0).then_inc(consts, 1)
            pool.wait_ge(consts, 4)
            pool.affine_select(out=routed[:, 0:1], in_=routed[:, 0:1], compare_op=ALU.is_ge, fill=0.0,
                               base=P - ROUTED_START, pattern=[[0, 1]], channel_multiplier=1)
            pool.affine_select(out=routed[:, 1:2], in_=routed[:, 1:2], compare_op=ALU.is_ge, fill=0.0,
                               base=ROUTED_END - 1 - (TPB - 1) * P, pattern=[[0, 1]], channel_multiplier=-1)\
                .then_inc(consts, 1)

            def root(n, slot):
                pool.wait_ge(var_ready, n + 1)
                pool.tensor_tensor(z_rstd[:], var[:], minus_half[:], ALU.pow).then_inc(z_rstd_ready, 1)

            root(0, 0)

            def step(batch, j):
                t = TPB * batch + j
                s = j % 2
                due = pool.compute_val(t + 1)
                pool.wait_ge(consts, 4)
                pool.wait_ge(mv_ready, due)
                pool.tensor_scalar(var_eps[:, s:s + 1], mean_var[:, s, 1:2], EPS, 1.0, ALU.add, ALU.mult)\
                    .then_inc(ve_ready, 1)
                pool.wait_ge(ve_ready, t + 1)
                pool.tensor_tensor(rstd[:, s:s + 1], var_eps[:, s:s + 1], minus_half[:, 0:1], ALU.pow)\
                    .then_inc(rstd_ready, 1)
                pool.wait_ge(consts, 4)
                pool.wait_ge(rstd_ready, due)
                pool.tensor_scalar(shift[:, s:s + 1], mean_var[:, s, 0:1], rstd[:, s:s + 1], -1.0,
                                   ALU.mult, ALU.mult).then_inc(shift_ready, 1)
                if j % TPU == 1:
                    next_unit(pool, batch, j, root)
            steps(pool, step)


def router_phase(nc, io, ident, q, coef):
    with ExitStack() as ctx:
        def sb(name, shape, dt=F32):
            return ctx.enter_context(nc.sbuf_tensor(f"R_{name}", shape, dt))

        def sem(name):
            return ctx.enter_context(nc.semaphore(f"R_{name}"))

        rw = sb("rw", [P, KC, EXPERTS])
        rb = sb("rb", [BATCHES, EXPERTS])
        logits = sb("logits", [BATCHES, EXPERTS])
        top = sb("top", [BATCHES, 1])
        weight = sb("weight", [BATCHES, EXPERTS])
        norm = sb("norm", [BATCHES, 1])
        wide = sb("wide", [BATCHES, EXPERTS, P // EXPERTS])
        ps_l = ctx.enter_context(nc.psum_tensor("R_ps_l", [BATCHES, EXPERTS], F32))
        ps_c = ctx.enter_context(nc.psum_tensor("R_ps_c", [P, BATCHES], F32))
        loaded = sem("loaded")
        product = sem("product")
        dve_done = sem("dve_done")
        shifted = sem("shifted")
        exp_done = sem("exp_done")
        wide_ready = sem("wide_ready")
        turned = sem("turned")
        block = ctx.enter_context(nc.Block())

        @block.sync
        def _(sp):
            sp.dma_start(rw[:], io["rw"]).then_inc(loaded, 16)
            sp.dma_start(rb[:], io["rb"].partition_broadcast(BATCHES)).then_inc(loaded, 16)

        @block.tensor
        def _(pe):
            pe.wait_ge(loaded, 32)
            for k in range(KC):
                last = pe.matmul(ps_l[:], q[:, k], rw[:, k], start=(k == 0), stop=(k == KC - 1))
            last.then_inc(product, 1)
            pe.wait_ge(wide_ready, 1)
            pe.transpose(ps_c[:], wide[:].rearrange("b e r -> b (e r)"), ident[:BATCHES, :BATCHES])\
              .then_inc(turned, 1)

        @block.scalar
        def _(act):
            act.wait_ge(shifted, 1)
            act.activation(weight[:], logits[:], ACT.Exp).then_inc(exp_done, 1)

        @block.vector
        def _(dve):
            done = [0]

            def after(ins):
                done[0] += 1
                ins.then_inc(dve_done, 1)
                dve.wait_ge(dve_done, done[0])

            dve.wait_ge(loaded, 32)
            dve.wait_ge(product, 1)
            after(dve.tensor_tensor(logits[:], ps_l[:], rb[:], ALU.add))
            after(dve.tensor_reduce(top[:], logits[:], AX, ALU.max))
            dve.tensor_scalar(logits[:], logits[:], top[:], None, ALU.subtract).then_inc(shifted, 1)
            dve.wait_ge(exp_done, 1)
            after(dve.tensor_reduce(norm[:], weight[:], AX, ALU.add))
            after(dve.reciprocal(norm[:], norm[:]))
            after(dve.tensor_scalar(weight[:], weight[:], norm[:], ROUTER_SCALE, ALU.mult, ALU.mult))
            dve.tensor_copy(wide[:], weight[:].unsqueeze(2).broadcast_to([BATCHES, EXPERTS, P // EXPERTS]))\
               .then_inc(wide_ready, 1)
            dve.wait_ge(turned, 1)
            after(dve.tensor_copy(coef[:, 0:BATCHES], ps_c[:]))
            dve.memset(coef[:, BATCHES:BATCHES + 1], 0.0)


def recycle_phase(nc, numbers):
    block = nc.Block()
    with block:
        @block.gpsimd
        def _(pool):
            pool.sem_clear(range(min(numbers), max(numbers) + 1))


def build(nc, a, out):
    semaphores = list(nc.free_semaphores)
    def scratch(name, shape):
        return nc.dram_tensor(name, shape, F32, kind="Internal").ap()

    x1 = scratch("x1_scratch", (TILES, P, D))
    x2 = scratch("x2_scratch", (TILES, P, D))
    x3 = scratch("x3_scratch", (TILES, P, D))
    h0 = scratch("h0_scratch", (P, TILES * P))
    with ExitStack() as ctx:
        def sb(name, shape, dt=F32):
            return ctx.enter_context(nc.sbuf_tensor(name, shape, dt))

        ident = sb("ident", [P, P])
        coef = sb("coef", [P, BATCHES + 1])
        bias_c = sb("bias_c", [P, LAYERS + 1])
        with ExitStack() as first:
            win_hi = first.enter_context(nc.sbuf_tensor("win_hi", [P, KC, P], F32R))
            win_lo = first.enter_context(nc.sbuf_tensor("win_lo", [P, KC, P], F32R))
            wall = first.enter_context(nc.sbuf_tensor("wall", [P, 2, 2, KC, D], F32R))
            persist = {"win_hi": win_hi, "win_lo": win_lo, "coef": coef, "bias_c": bias_c}
            setup_phase(nc, a, wall, ident, persist)
            dense_phase(nc, "A", {"x": a["x_t"], "out": x1}, wall, ident)
            dense_phase(nc, "B", {"x": x1, "out": x2, "w": a["w1_t"], "bias": a["bias1"], "rank": 48,
                                  "a": a["lora_a"], "b_t": a["lora_bt"], "coef": coef[:48], "win_hi": win_hi,
                                  "win_lo": win_lo, "bin": bias_c[:, 0:1], "h": h0}, wall, ident)
        recycle_phase(nc, semaphores)
        q = sb("q", [P, KC, BATCHES])
        with ExitStack() as second:
            def sb1(name, shape, dt=F32):
                return second.enter_context(nc.sbuf_tensor(name, shape, dt))

            m = {"vec": sb1("vec", [P, len(VECS), LAYERS]), "rho": sb1("rho", [P, LAYERS]),
                 "b1": sb1("b1", [P, LAYERS, FCH]), "wout": sb1("wout", [P, D]), "ones": sb1("ones", [1, P], F32R),
                 "wout_hi": sb1("wout_hi", [P, D], F32R), "wout_lo": sb1("wout_lo", [P, D], F32R),
                 "row_hi": sb1("row_hi", [1, D], F32R), "row_lo": sb1("row_lo", [1, D], F32R),
                 "h": sb1("h", [P, TILES * P]), "b2": bias_c[:, 1:]}
            with ExitStack() as small:
                def sb2(name, shape, dt=F32):
                    return small.enter_context(nc.sbuf_tensor(name, shape, dt))

                m["w1"] = sb2("w1", [P, LAYERS, FCH * P])
                m["w2"] = sb2("w2", [P, LAYERS, FCH, P])
                m["w2_flat"] = m["w2"][:].rearrange("p l q d -> p l (q d)")
                m["mix"] = sb2("mix", [P, LAYERS, P])
                m["table"] = sb2("table", [P, 2, LAYERS, SEQ])
                prepare_phase(nc, a, ident, m)
                small_model_phase(nc, {"h": h0}, ident, m)
            readout_phase(nc, {"x": x2, "out": x3}, ident, m, q)
        router_phase(nc, {"rw": a["router_w"], "rb": a["router_b"]}, ident, q, coef)
        with ExitStack() as third:
            wall = third.enter_context(nc.sbuf_tensor("wall_d", [P, 2, 2, KC, D], F32R))
            dense_phase(nc, "D", {"x": x3, "out": out, "w": a["w3_t"], "bias": a["bias3"], "rank": P,
                                  "a": a["expert_a"], "b_t": a["expert_bt"], "coef": coef}, wall, ident)


def kernel(**inputs):
    import numpy as np
    import concourse.bacc as bacc
    from concourse.bass_utils import run_bass_kernel_spmd as run

    def arr(name):
        return np.asarray(inputs[name])

    laid = {
        "x_t": arr("L0_attn_data").reshape(TILES, P, KC, P).transpose(0, 3, 2, 1).reshape(TILES, P, D),
        "w0_t": arr("L0_attn_weight").T.reshape(KC, P, D),
        "mask_t": arr("L0_attn_mask").T.reshape(KC, P, D),
        "w1_t": arr("L0_ffn_weight").T.reshape(KC, P, D),
        "bias1": arr("L0_ffn_bias"),
        "lora_a": arr("L0_ffn_lora_A").reshape(48, D),
        "lora_bt": arr("L0_ffn_lora_B").transpose(0, 2, 1).reshape(48, D),
        "starts": arr("L0_ffn_lora_start_indices"),
        "win_t": arr("L1_attn_Win").T.reshape(KC, P, P).transpose(1, 0, 2),
        "vec": np.stack([arr(f"L1_attn_{n}").T for n in VECS], axis=1),
        "mlp1_t": arr("L1_attn_W1").transpose(2, 0, 1),
        "mlp2_t": arr("L1_attn_W2").reshape(LAYERS, P, FCH, P).transpose(3, 0, 2, 1),
        "mlp_b1": arr("L1_attn_b1").reshape(LAYERS, FCH, P).transpose(2, 0, 1),
        "lnl": np.stack([arr("L1_attn_lnl_w"), arr("L1_attn_lnl_b")], axis=1),
        "wout_t": arr("L1_attn_Wout").T,
        "bout": arr("L1_attn_bout")[None],
        "router_w": arr("L1_ffn_router_W").T.reshape(KC, P, EXPERTS).transpose(1, 0, 2),
        "router_b": arr("L1_ffn_router_b"),
        "w3_t": arr("L1_ffn_W").T.reshape(KC, P, D),
        "bias3": arr("L1_ffn_b"),
        "expert_a": arr("L1_ffn_A").reshape(P, D),
        "expert_bt": arr("L1_ffn_B").transpose(0, 2, 1).reshape(P, D),
        "bias_stack": np.concatenate([arr("L1_attn_bin")[:, None], arr("L1_attn_b2").T], axis=1),
    }
    nc = bacc.Bacc("TRN2", target_bir_lowering=False, num_devices=1)
    arrays, a = {}, {}
    for name, x in laid.items():
        arrays[f"in_{name}"] = np.ascontiguousarray(x)
        a[name] = nc.dram_tensor(f"in_{name}", x.shape, mybir.dt.from_np(x.dtype), kind="ExternalInput").ap()
    out = nc.dram_tensor("out_0", (TILES, P, D), F32, kind="ExternalOutput").ap()
    build(nc, a, out)
    r = run(nc, [arrays], core_ids=[0])
    return r.results[0]["out_0"].reshape(BATCHES, SEQ, D)
```

```python
from contextlib import ExitStack, nullcontext
from itertools import groupby

import concourse.bass as bass
from concourse import mybir

P = 128
D = 1024
KC = D // P
HALF = 512
BATCHES = 4
SEQ = 1024
TILES = BATCHES * SEQ // P
TPB = SEQ // P
BODY = 2 * TPB
EPS = 1e-5
LAYERS = 4
FCH = 4
UNITS = BATCHES * SEQ // HALF
LAG = 7
ROWS = 33
EXPERTS = 8
ROUTER_SCALE = 2.0
ROUTED_START = 34 + 144 + 1
ROUTED_END = SEQ - 1

F32 = mybir.dt.float32
F32R = mybir.dt.float32r
I32 = mybir.dt.int32
ALU = mybir.AluOpType
ACT = mybir.ActivationFunctionType
AX = mybir.AxisListType.X


def dense_phase(nc, kind, io, walls, ident, prepare=None, router=None):
    low_rank = kind in "BD"
    project = kind == "B"
    rank = io["rank"] if low_rank else 0
    with ExitStack() as ctx:
        def sb(name, shape, dt=F32):
            return ctx.enter_context(nc.sbuf_tensor(f"{kind}_{name}", shape, dt))

        def psum(name, shape):
            return ctx.enter_context(nc.psum_tensor(f"{kind}_{name}", shape, F32))

        def sem(name):
            return ctx.enter_context(nc.semaphore(f"{kind}_{name}"))

        x_in = sb("x_in", [P, D])
        x_hi = sb("x_hi", [P, 2, KC, P], F32R)
        x_lo = sb("x_lo", [P, 2, KC, P], F32R)
        row = sb("row", [P, 2, D])
        stats = sb("stats", [P, 2, 2, 6])
        mean_var = sb("mean_var", [P, 2, 2])
        var_eps = sb("var_eps", [P, 2])
        rstd = sb("rstd", [P, 2])
        shift = sb("shift", [P, 2])
        minus_half = sb("minus_half", [P, 1])
        ps_out = [psum(f"ps_out{h}", [P, HALF]) for h in range(2)]
        if low_rank:
            bias = sb("bias", [P, D])
            a_in = sb("a_in", [rank, 2, P])
            a_hi = sb("a_hi", [rank, 2, P], F32R)
            a_lo = sb("a_lo", [rank, 2, P], F32R)
            b_in = sb("b_in", [rank, D])
            b_hi = sb("b_hi", [rank, D], F32R)
            b_lo = sb("b_lo", [rank, D], F32R)
            w_in = sb("w_in", [P, 2, HALF])
            forwarded = sb("forwarded", [P, 2])
            ps_x = psum("ps_x", [P, D])
            ps_w = psum("ps_w", [P, HALF])
        if project:
            y_hi = sb("y_hi", [P, KC, 2 * P], F32R)
            y_lo = sb("y_lo", [P, KC, 2 * P], F32R)
            h_out = sb("h_out", [P, 2, 2 * P])
            ps_y = psum("ps_y", [P, D])
            ps_h = psum("ps_h", [P, 2 * P])

        x_loaded = sem("x_loaded")
        x_turned = sem("x_turned")
        hi_ready = sem("hi_ready")
        lo_ready = sem("lo_ready")
        mm_done = sem("mm_done")
        evacuated = [sem(f"evacuated{h}") for h in range(2)]
        stats_ready = sem("stats_ready")
        mv_ready = sem("mv_ready")
        ve_ready = sem("ve_ready")
        rstd_ready = sem("rstd_ready")
        shift_ready = sem("shift_ready")
        normed = sem("normed")
        stored = [sem(f"stored{s}") for s in range(2)]
        const_ready = sem("const_ready")
        bias_loaded = sem("bias_loaded")
        a_loaded = [sem(f"a_loaded{o}") for o in range(2)]
        a_hi_ready = sem("a_hi_ready")
        a_lo_ready = sem("a_lo_ready")
        bt_loaded = sem("bt_loaded")
        b_hi_ready = sem("b_hi_ready")
        b_lo_ready = sem("b_lo_ready")
        w_loaded = [sem(f"w_loaded{o}") for o in range(2)]
        raw_loaded = [sem(f"raw_loaded{i}") for i in range(6)]
        w_diag = sem("w_diag")
        w_product = sem("w_product")
        w_summed = sem("w_summed")
        w_hi_ready = sem("w_hi_ready")
        w_lo_ready = sem("w_lo_ready")
        first_lo_ready = sem("first_lo_ready")
        y_turned = sem("y_turned")
        y_hi_ready = sem("y_hi_ready")
        y_lo_ready = sem("y_lo_ready")
        h_done = sem("h_done")
        h_evacuated = sem("h_evacuated")
        h_stored = [sem(f"h_stored{s}") for s in range(2)]

        def steps(eng, step):
            with eng.Fori(0, TILES // BODY) as turn:
                for j in range(BODY):
                    step(turn, j)

        def only_in(eng, which, guarded, turn):
            return (eng.If(turn < 1 if which == 0 else turn > 0), which) if guarded else (nullcontext(), turn)

        PARTS = 2 * KC

        def place(u):
            k, o = u % KC, u // KC
            return k, slice(o * HALF, (o + 1) * HALF), o == k * P // HALF

        RAW = 6

        def raw(batch, u):
            if isinstance(batch, int) and batch == 0:
                slot = u % RAW
                return w_in[:, slot] if slot < 2 else \
                    row[:, (slot - 2) // 2, (slot - 2) % 2 * HALF:((slot - 2) % 2 + 1) * HALF]
            return w_in[:, u % 2]

        def part_bank(batch, u):
            return ps_out[1] if isinstance(batch, int) and batch == 0 and u % 2 else ps_w

        def weights_next(eng, turn, j, i, part):
            if low_rank:
                guard, now = only_in(eng, 0, j >= TPB, turn)
                with guard:
                    part(2 * now + j // TPB + 1, (j // TPB + 1) % 2, 2 * (j % TPB) + i)

        def beside(eng, turn, part):
            if prepare:
                with eng.If(turn < 1):
                    part()

        def weights_first(eng, turn, j, make_parts):
            if low_rank and j == 0:
                with eng.If(turn < 1):
                    make_parts(range(KC, PARTS))

        block = ctx.enter_context(nc.Block())

        @block.sync
        def _(sp):
            def load_x(t):
                if low_rank:
                    sp.wait_ge(x_turned, t)
                else:
                    sp.wait_ge(hi_ready, t)
                    sp.wait_ge(lo_ready, t)
                sp.dma_start(x_in[:], io["x"][t]).then_inc(x_loaded, 16)

            def load_part(batch, par, u):
                n = PARTS * batch + u
                k, cols, _ = place(u)
                if not (isinstance(batch, int) and n < 2):
                    sp.wait_ge(a_hi_ready, n - 1)
                    sp.wait_ge(a_lo_ready, n - 1)
                sp.dma_start(a_in[:, u % 2], io["a"][:, k * P:(k + 1) * P]).then_inc(a_loaded[u % 2], 16)
                if isinstance(batch, int) and batch == 0:
                    if u >= RAW:
                        sp.wait_ge(w_hi_ready, u - RAW + 1)
                        sp.wait_ge(first_lo_ready, u - RAW + 1)
                    sp.dma_start(raw(0, u), io["w"][k][:, cols]).then_inc(raw_loaded[u % RAW], 16)
                else:
                    sp.wait_ge(w_hi_ready, n - 1)
                    sp.wait_ge(w_lo_ready, n - 1)
                    sp.dma_start(w_in[:, u % 2], io["w"][k][:, cols]).then_inc(w_loaded[u % 2], 16)

            def load_parts(parts):
                for u in parts:
                    load_part(0, 0, u)

            if router:
                router.load(sp)
            load_x(0)
            if low_rank:
                load_parts(range(1))
                sp.dma_start(b_in[:], io["b_t"]).then_inc(bt_loaded, 16)
                load_parts(range(1, KC))
                sp.dma_start(bias[:], io["bias"].partition_broadcast(P)).then_inc(bias_loaded, 16)
            load_x(1)
            if prepare:
                prepare.load(sp)

            def step(turn, j):
                if prepare and j == 1:
                    with sp.If(turn > 0):
                        prepare.store(sp)
                weights_first(sp, turn, j, load_parts)
                for i in range(2):
                    weights_next(sp, turn, j, i, load_part)
                guard, now = only_in(sp, 0, j >= BODY - 2, turn)
                with guard:
                    load_x(BODY * now + j + 2)

            steps(sp, step)
            if prepare:
                prepare.wait_stored(sp)

        @block.tensor
        def _(pe):
            def turn_x(t):
                pe.wait_ge(x_loaded, 16 * (t + 1))
                pe.wait_ge(hi_ready, t)
                pe.wait_ge(lo_ready, t)
                for k in range(KC):
                    last = pe.transpose(ps_x[:, k * P:(k + 1) * P], x_in[:, k * P:(k + 1) * P], ident[:])
                last.then_inc(x_turned, 1)

            def product(t, j, par, h):
                if h == 0:
                    pe.wait_ge(hi_ready, t + 1)
                    pe.wait_ge(lo_ready, t + 1)
                pe.wait_ge(evacuated[h], t)
                cols = slice(h * HALF, (h + 1) * HALF)
                s = j % 2
                for k in range(KC):
                    pe.matmul(ps_out[h][:], x_hi[:, s, k], walls[par][:, 0, k, cols], start=(k == 0), stop=False)
                    pe.matmul(ps_out[h][:], x_hi[:, s, k], walls[par][:, 1, k, cols], start=False, stop=False)
                    last = pe.matmul(ps_out[h][:], x_lo[:, s, k], walls[par][:, 0, k, cols],
                                     start=False, stop=(k == KC - 1))
                last.then_inc(mm_done, 1)

            def weight_part(batch, par, u):
                n = PARTS * batch + u
                pe.wait_ge(a_hi_ready, n + 1)
                pe.wait_ge(a_lo_ready, n + 1)
                if u == 0:
                    pe.wait_ge(b_hi_ready, 2 * batch + 2)
                    pe.wait_ge(b_lo_ready, 2 * batch + 2)
                if isinstance(batch, int) and batch == 0:
                    if u >= 2:
                        pe.wait_ge(w_summed, u - 1)
                else:
                    pe.wait_ge(w_summed, n)
                _, cols, _ = place(u)
                s, bank = u % 2, part_bank(batch, u)
                pe.matmul(bank[:], a_hi[:, s], b_hi[:, cols], start=True, stop=False)
                pe.matmul(bank[:], a_hi[:, s], b_lo[:, cols], start=False, stop=False)
                pe.matmul(bank[:], a_lo[:, s], b_hi[:, cols], start=False, stop=True).then_inc(w_product, 1)

            def turn_y(t, j):
                pe.wait_ge(normed, t + 1)
                pe.wait_ge(y_hi_ready, t + 1)
                pe.wait_ge(y_lo_ready, t + 1)
                for k in range(KC):
                    last = pe.transpose(ps_y[:, k * P:(k + 1) * P], row[:, j % 2, k * P:(k + 1) * P], ident[:])
                last.then_inc(y_turned, 1)

            def project_pair(pair):
                pe.wait_ge(y_hi_ready, 2 * pair + 3)
                pe.wait_ge(y_lo_ready, 2 * pair + 3)
                pe.wait_ge(h_evacuated, pair + 1)
                for k in range(KC):
                    pe.matmul(ps_h[:], io["win_hi"][:, k], y_hi[:, k], start=(k == 0), stop=False)
                    pe.matmul(ps_h[:], io["win_hi"][:, k], y_lo[:, k], start=False, stop=False)
                    last = pe.matmul(ps_h[:], io["win_lo"][:, k], y_hi[:, k], start=False, stop=(k == KC - 1))
                last.then_inc(h_done, 1)

            def make_parts(parts):
                for u in parts:
                    weight_part(0, 0, u)

            if router:
                router.tensor_part(pe)
            if low_rank:
                turn_x(0)
                make_parts(range(KC))

            def step(turn, j):
                t = BODY * turn + j
                batch = 2 * turn + j // TPB
                if low_rank:
                    guard, now = only_in(pe, 0, j == BODY - 1, turn)
                    with guard:
                        turn_x(BODY * now + j + 1)
                    if j % TPB == 0:
                        pe.wait_ge(w_hi_ready, PARTS * batch + KC)
                        pe.wait_ge(w_lo_ready, PARTS * batch + KC)
                par = (j // TPB) % 2 if low_rank else 1
                product(t, j, par, 0)
                if j == 2:
                    beside(pe, turn, lambda: prepare.tensor_part(pe))
                if project and j % 2:
                    guard, now = only_in(pe, 1, j == 1, turn)
                    with guard:
                        project_pair(TPB * now + (j - 3) // 2)
                weights_first(pe, turn, j, make_parts)
                if low_rank and j % TPB == 0:
                    pe.wait_ge(w_hi_ready, PARTS * batch + PARTS)
                    pe.wait_ge(w_lo_ready, PARTS * batch + PARTS)
                weights_next(pe, turn, j, 0, weight_part)
                product(t, j, par, 1)
                weights_next(pe, turn, j, 1, weight_part)
                if project:
                    guard, now = only_in(pe, 1, j == 0, turn)
                    with guard:
                        turn_y(BODY * now + j - 1, j + 1)

            steps(pe, step)
            if project:
                turn_y(TILES - 1, 1)
                project_pair(TILES // 2 - 1)

        @block.scalar
        def _(act):
            def split_x(t, j):
                if low_rank:
                    act.wait_ge(x_turned, t + 1)
                else:
                    act.wait_ge(x_loaded, 16 * (t + 1))
                if not (isinstance(t, int) and t < 2):
                    act.wait_ge(mm_done, 2 * (t - 1))
                src = ps_x if low_rank else x_in
                act.activation(x_hi[:, j % 2].rearrange("p k t -> p (k t)"), src[:], ACT.Identity)\
                   .then_inc(hi_ready, 1)

            def split_a(batch, par, u):
                n = PARTS * batch + u
                act.wait_ge(a_loaded[u % 2], 16 * (KC * batch + u // 2 + 1))
                if not (isinstance(batch, int) and n < 2):
                    act.wait_ge(w_product, n - 1)
                act.activation(a_hi[:, u % 2], a_in[:, u % 2], ACT.Identity).then_inc(a_hi_ready, 1)
                if u == 0:
                    split_b(batch)

            def split_b(batch):
                for o in range(2):
                    free = act.compute_val(PARTS * batch)
                    act.wait_ge(bt_loaded, 16)
                    act.wait_ge(w_product, free)
                    coef = io["coef"][:, batch:batch + 1] if isinstance(batch, int)\
                        else io["coef"][:, bass.ds(batch, 1)]
                    act.activation(b_hi[:, o * HALF:(o + 1) * HALF], b_in[:, o * HALF:(o + 1) * HALF],
                                   ACT.Identity, scale=coef).then_inc(b_hi_ready, 1)

            def weight_hi(batch, par, u):
                k, cols, _ = place(u)
                act.wait_ge(w_summed, PARTS * batch + u + 1)
                act.activation(walls[par][:, 0, k, cols], raw(batch, u), ACT.Identity).then_inc(w_hi_ready, 1)

            def make_parts(parts):
                for u in parts:
                    if u == parts[0]:
                        split_a(0, 0, u)
                    if u != parts[-1]:
                        split_a(0, 0, u + 1)
                    if u != parts[0]:
                        weight_hi(0, 0, u - 1)
                weight_hi(0, 0, parts[-1])

            def evacuate(turn, j, h):
                t = BODY * turn + j
                act.wait_ge(mm_done, 2 * t + h + 1)
                act.wait_ge(stored[j % 2], 16 * (TPB * turn + j // 2))
                act.activation(row[:, j % 2, h * HALF:(h + 1) * HALF], ps_out[h][:], ACT.Identity)\
                   .then_inc(evacuated[h], 1)

            def normalise(t, j):
                s = j % 2
                act.wait_ge(shift_ready, t + 1)
                act.activation(row[:, s], row[:, s], ACT.Identity, bias=shift[:, s:s + 1],
                               scale=rstd[:, s:s + 1]).then_inc(normed, 1)
                act.wait_ge(normed, t + 1)
                act.dma_start(io["out"][t], row[:, s]).then_inc(stored[s], 16)

            def split_y(t, j):
                act.wait_ge(y_turned, t + 1)
                act.activation(y_hi[:, :, (j % 2) * P:(j % 2 + 1) * P],
                               ps_y[:].rearrange("p (k t) -> p k t", k=KC), ACT.Identity)\
                   .then_inc(y_hi_ready, 1)

            def evacuate_h(turn, j):
                q = (j - 3) // 2
                slot = q % 2
                pair = TPB * turn + q
                act.wait_ge(h_done, pair + 1)
                act.wait_ge(h_stored[slot], 16 * (TPB // 2 * turn + q // 2 + 1))
                act.activation(h_out[:, slot], ps_h[:], ACT.Identity, bias=io["bin"][:]).then_inc(h_evacuated, 1)
                act.wait_ge(h_evacuated, pair + 2)
                act.dma_start(io["h"][:, bass.ds(2 * P * pair, 2 * P)] if not isinstance(pair, int)
                              else io["h"][:, 2 * P * pair:2 * P * (pair + 1)], h_out[:, slot])\
                   .then_inc(h_stored[slot], 16)

            if router:
                router.scalar_part(act)
                act.wait_ge(router.coef_ready, 1)
            split_x(0, 0)
            if low_rank:
                make_parts(range(KC))

            def step(turn, j):
                t = BODY * turn + j
                guard, now = only_in(act, 0, j == BODY - 1, turn)
                with guard:
                    split_x(BODY * now + j + 1, j + 1)
                weights_first(act, turn, j, make_parts)
                weights_next(act, turn, j, 0, split_a)
                weights_next(act, turn, j, 1, split_a)
                guard, now = only_in(act, 1, j == 0, turn)
                with guard:
                    normalise(BODY * now + j - 1, j + 1)

                weights_next(act, turn, j, 0, weight_hi)
                if not low_rank:
                    evacuate(turn, j, 0)
                if project and j % 2:
                    guard, now = only_in(act, 1, j == 1, turn)
                    with guard:
                        evacuate_h(now, j)
                weights_next(act, turn, j, 1, weight_hi)
                if project:
                    guard, now = only_in(act, 1, j == 0, turn)
                    with guard:
                        split_y(BODY * now + j - 1, j + 1)
                if not low_rank:
                    evacuate(turn, j, 1)
                if j == 1:
                    beside(act, turn, lambda: prepare.scalar_part(act))

            steps(act, step)
            normalise(TILES - 1, 1)
            if project:
                split_y(TILES - 1, 1)
                evacuate_h(TILES // BODY, 1)
                for s in range(2):
                    act.wait_ge(h_stored[s], 16 * (TILES // 4 + 1))
            for s in range(2):
                act.wait_ge(stored[s], 16 * TILES // 2)

        @block.vector
        def _(dve):
            if project:
                nc.vector.memset(stats[:, 0, 0, 0:1], 0.0).then_inc(y_hi_ready, 1)
                nc.vector.memset(stats[:, 0, 0, 1:2], 0.0).then_inc(y_lo_ready, 1)
                nc.vector.memset(stats[:, 0, 0, 2:3], 0.0).then_inc(h_evacuated, 1)
                nc.vector.memset(stats[:, 0, 0, 3:4], 0.0).then_inc(h_stored[0], 16)
                nc.vector.memset(stats[:, 0, 0, 4:5], 0.0).then_inc(h_stored[1], 16)

            def split_x(t, j):
                dve.wait_ge(hi_ready, t + 1)
                src = ps_x if low_rank else x_in
                s = j % 2
                dve.tensor_tensor(x_lo[:, s].rearrange("p k t -> p (k t)"), src[:],
                                  x_hi[:, s].rearrange("p k t -> p (k t)").bitcast(F32), ALU.subtract)\
                   .then_inc(lo_ready, 1)

            def split_a(batch, par, u):
                dve.wait_ge(a_hi_ready, PARTS * batch + u + 1)
                dve.tensor_tensor(a_lo[:, u % 2], a_in[:, u % 2], a_hi[:, u % 2].bitcast(F32), ALU.subtract)\
                   .then_inc(a_lo_ready, 1)
                if u == 0:
                    split_b(batch)

            def split_b(batch):
                for o in range(2):
                    cols = slice(o * HALF, (o + 1) * HALF)
                    dve.wait_ge(b_hi_ready, 2 * batch + o + 1)
                    coef = io["coef"][:, batch:batch + 1] if isinstance(batch, int)\
                        else io["coef"][:, bass.ds(batch, 1)]
                    dve.scalar_tensor_tensor(b_lo[:, cols], b_in[:, cols], coef, b_hi[:, cols].bitcast(F32),
                                             ALU.mult, ALU.subtract).then_inc(b_lo_ready, 1)

            def weight_sum(batch, par, u):
                k, cols, diagonal = place(u)
                part = raw(batch, u)
                if isinstance(batch, int) and batch == 0:
                    dve.wait_ge(raw_loaded[u % RAW], 16 * (u // RAW + 1))
                else:
                    dve.wait_ge(w_loaded[u % 2], 16 * (KC * batch + u // 2 + 1 - KC))
                if diagonal:
                    diag = part[:, k * P - cols.start:(k + 1) * P - cols.start]
                    dve.tensor_tensor(diag, diag, ident[:], ALU.add).then_inc(w_diag, 1)
                    dve.wait_ge(w_diag, KC * batch + k + 1)
                dve.wait_ge(w_product, PARTS * batch + u + 1)
                dve.tensor_tensor(part, part_bank(batch, u)[:], part, ALU.add).then_inc(w_summed, 1)

            def weight_lo(batch, par, u):
                k, cols, _ = place(u)
                dve.wait_ge(w_hi_ready, PARTS * batch + u + 1)
                dve.tensor_tensor(walls[par][:, 1, k, cols], raw(batch, u), walls[par][:, 0, k, cols].bitcast(F32),
                                  ALU.subtract).then_inc(w_lo_ready, 1)

            def make_parts(parts):
                for u in parts:
                    if u == parts[0]:
                        split_a(0, 0, u)
                    if u != parts[-1]:
                        split_a(0, 0, u + 1)
                    weight_sum(0, 0, u)
                dve.wait_ge(first_lo_ready, parts[-1] + 1)
                dve.memset(forwarded[:, parts[0] // KC:parts[0] // KC + 1], 0.0).then_inc(w_lo_ready, len(parts))

            def half_stats(turn, j, h):
                t = BODY * turn + j
                s = j % 2
                cols = slice(h * HALF, (h + 1) * HALF)
                if low_rank:
                    dve.wait_ge(mm_done, 2 * t + h + 1)
                    dve.wait_ge(stored[s], 16 * (TPB * turn + j // 2))
                    dve.tensor_tensor(row[:, s, cols], ps_out[h][:], bias[:, cols], ALU.add)\
                       .then_inc(evacuated[h], 1)
                dve.wait_ge(evacuated[h], t + 1)
                dve.bn_stats(stats[:, s, h], row[:, s, cols]).then_inc(stats_ready, 1)

            def aggregate(t, j):
                s = j % 2
                due = dve.compute_val(2 * t + 2)
                dve.wait_ge(const_ready, 1)
                dve.wait_ge(stats_ready, due)
                dve.bn_aggr(mean_var[:, s], stats[:, s].rearrange("p a b -> p (a b)")).then_inc(mv_ready, 1)

            def split_y(t, j):
                dve.wait_ge(y_hi_ready, t + 2)
                cols = slice((j % 2) * P, (j % 2 + 1) * P)
                dve.tensor_tensor(y_lo[:, :, cols], ps_y[:].rearrange("p (k t) -> p k t", k=KC),
                                  y_hi[:, :, cols].bitcast(F32), ALU.subtract).then_inc(y_lo_ready, 1)

            if router:
                router.vector_part(dve)
            split_x(0, 0)
            if low_rank:
                make_parts(range(KC))
                dve.wait_ge(bias_loaded, 16)

            def step(turn, j):
                t = BODY * turn + j
                if j == 0:
                    guard, now = only_in(dve, 1, True, turn)
                    with guard:
                        half_stats(now - 1, BODY - 1, 1)
                        aggregate(BODY * now - 1, 1)
                else:
                    half_stats(turn, j - 1, 1)
                    aggregate(t - 1, j - 1)
                guard, now = only_in(dve, 0, j == BODY - 1, turn)
                with guard:
                    split_x(BODY * now + j + 1, j + 1)

                weights_first(dve, turn, j, make_parts)
                weights_next(dve, turn, j, 0, split_a)
                weights_next(dve, turn, j, 1, split_a)
                half_stats(turn, j, 0)
                for i in range(2):
                    weights_next(dve, turn, j, i, weight_sum)
                    weights_next(dve, turn, j, i, weight_lo)
                if project:
                    guard, now = only_in(dve, 1, j == 0, turn)
                    with guard:
                        split_y(BODY * now + j - 1, j + 1)
                beside(dve, turn, lambda: prepare.vector_part(dve, j))

            steps(dve, step)
            half_stats(TILES // BODY - 1, BODY - 1, 1)
            aggregate(TILES - 1, 1)
            if project:
                split_y(TILES - 1, 1)

        @block.gpsimd
        def _(pool):
            pool.memset(minus_half[:], -0.5).then_inc(const_ready, 1)
            pool.wait_ge(const_ready, 1)
            if prepare:
                prepare.pool_part(pool)
            if low_rank:
                for u in range(PARTS):
                    k, cols, _ = place(u)
                    pool.wait_ge(w_hi_ready, u + 1)
                    pool.tensor_tensor(walls[0][:, 1, k, cols], raw(0, u), walls[0][:, 0, k, cols].bitcast(F32),
                                       ALU.subtract).then_inc(first_lo_ready, 1)
            with pool.Fori(0, TILES // 2) as pair:
                for s in range(2):
                    t = 2 * pair + s
                    due = pool.compute_val(t + 1)
                    pool.wait_ge(const_ready, 1)
                    pool.wait_ge(mv_ready, due)
                    pool.tensor_scalar(var_eps[:, s:s + 1], mean_var[:, s, 1:2], EPS, 1.0, ALU.add, ALU.mult)\
                        .then_inc(ve_ready, 1)
                    pool.wait_ge(ve_ready, t + 1)
                    pool.tensor_tensor(rstd[:, s:s + 1], var_eps[:, s:s + 1], minus_half[:], ALU.pow)\
                        .then_inc(rstd_ready, 1)
                    pool.wait_ge(const_ready, 1)
                    pool.wait_ge(rstd_ready, due)
                    pool.tensor_scalar(shift[:, s:s + 1], mean_var[:, s, 0:1], rstd[:, s:s + 1], -1.0,
                                       ALU.mult, ALU.mult).then_inc(shift_ready, 1)


def setup_phase(nc, io, walls, ident, persist):
    with ExitStack() as ctx:
        def sb(name, shape, dt=F32):
            return ctx.enter_context(nc.sbuf_tensor(f"S_{name}", shape, dt))

        def sem(name):
            return ctx.enter_context(nc.semaphore(f"S_{name}"))

        NB = D // 32
        w_in = sb("w_in", [P, KC, D])
        m_in = sb("m_in", [P, KC, D], I32)
        block_sum = sb("block_sum", [P, 2, NB])
        block_on = sb("block_on", [P, 2, NB])
        same_block = sb("same_block", [P, P])
        centre = sb("centre", [P, P])
        win_in = sb("win_in", [P, KC, P])
        win_mean = sb("win_mean", [P, KC])
        bias_in = sb("bias_in", [P, LAYERS + 1])
        starts = sb("starts", [48, 4], I32)
        below = sb("below", [48, 4, 4])
        count = sb("count", [48, 4])
        adapter = sb("adapter", [48, 2])
        ps_block = [ctx.enter_context(nc.psum_tensor(f"S_ps_block{s}", [P, NB], F32)) for s in range(2)]
        ps_bias = ctx.enter_context(nc.psum_tensor("S_ps_bias", [P, LAYERS + 1], F32))

        consts = sem("consts")
        ident_ready = sem("ident_ready")
        w_loaded = [sem(f"w_loaded{k}") for k in range(KC)]
        m_loaded = [sem(f"m_loaded{k}") for k in range(KC)]
        small_loaded = sem("small_loaded")
        summed = sem("summed")
        spread = sem("spread")
        on_ready = sem("on_ready")
        masked = sem("masked")
        diag_ready = sem("diag_ready")
        hi_ready = sem("hi_ready")
        lo_ready = sem("lo_ready")
        dve_done = sem("dve_done")
        win_ready = sem("win_ready")
        win_hi_ready = sem("win_hi_ready")
        centre_ready = sem("centre_ready")
        bias_done = sem("bias_done")
        adapter_parts = sem("adapter_parts")

        block = ctx.enter_context(nc.Block())

        @block.sync
        def _(sp):
            for k in range(KC):
                sp.dma_start(m_in[:, k], io["mask_t"][k]).then_inc(m_loaded[k], 16)
                sp.dma_start(w_in[:, k], io["w0_t"][k]).then_inc(w_loaded[k], 16)

        @block.scalar
        def _(act):
            act.dma_start(win_in[:], io["win_t"]).then_inc(small_loaded, 16)
            act.dma_start(bias_in[:], io["bias_stack"]).then_inc(small_loaded, 16)
            act.dma_start(starts[:], io["starts"].partition_broadcast(48)).then_inc(small_loaded, 16)
            for k in range(KC):
                act.wait_ge(diag_ready, k + 1)
                act.activation(walls[1][:, 0, k], w_in[:, k], ACT.Identity).then_inc(hi_ready, 1)
            act.wait_ge(win_ready, 1)
            act.activation(persist["win_hi"][:].rearrange("p k d -> p (k d)"),
                           win_in[:].rearrange("p k d -> p (k d)"), ACT.Identity).then_inc(win_hi_ready, 1)

        @block.gpsimd
        def _(pool):
            pool.memset(ident[:], 0.0).then_inc(consts, 1)
            pool.memset(same_block[:], 0.0).then_inc(consts, 1)
            pool.memset(adapter[:], 1.0).then_inc(consts, 1)
            pool.wait_ge(consts, 3)
            for i in range(P // 32):
                pool.memset(same_block[32 * i:32 * i + 32, 32 * i:32 * i + 32], 1.0).then_inc(consts, 1)
            pool.wait_ge(consts, 3 + P // 32)
            pool.affine_select(out=ident[:], in_=ident[:], compare_op=ALU.not_equal, fill=1.0, base=0,
                               pattern=[[-1, P]], channel_multiplier=1).then_inc(ident_ready, 1)
            for i in range(2):
                pool.affine_select(out=adapter[:, i:i + 1], in_=adapter[:, i:i + 1], compare_op=ALU.is_ge,
                                   fill=0.0, base=-16 * (i + 1), pattern=[[0, 1]], channel_multiplier=1)\
                    .then_inc(adapter_parts, 1)
            for k in range(KC):
                s = k % 2
                pool.wait_ge(on_ready, k + 1)
                pool.wait_ge(w_loaded[k], 16)
                w = w_in[:, k].rearrange("p (n c) -> p n c", n=NB)
                pool.tensor_tensor(w, w, block_on[:, s].unsqueeze(2).broadcast_to([P, NB, 32]), ALU.mult)\
                    .then_inc(masked, 1)

        @block.tensor
        def _(pe):
            pe.wait_ge(consts, 3 + P // 32)
            for k in range(KC):
                s = k % 2
                pe.wait_ge(summed, k + 1)
                if k >= 2:
                    pe.wait_ge(on_ready, k - 1)
                pe.matmul(ps_block[s][:], same_block[:], block_sum[:, s], start=True, stop=True).then_inc(spread, 1)
            pe.wait_ge(centre_ready, 1)
            pe.wait_ge(small_loaded, 48)
            pe.matmul(ps_bias[:], centre[:], bias_in[:], start=True, stop=True).then_inc(bias_done, 1)

        @block.vector
        def _(dve):
            def block_sums(k):
                s = k % 2
                dve.wait_ge(m_loaded[k], 16)
                if k >= 2:
                    dve.wait_ge(spread, k - 1)
                dve.tensor_reduce(block_sum[:, s], m_in[:, k].rearrange("p (n c) -> p n c", n=NB), AX, ALU.add)\
                   .then_inc(summed, 1)

            def compare(k):
                s = k % 2
                dve.wait_ge(spread, k + 1)
                if k >= 2:
                    dve.wait_ge(masked, k - 1)
                dve.tensor_scalar(block_on[:, s], ps_block[s][:], 0.0, None, ALU.is_gt).then_inc(on_ready, 1)

            def finish(k):
                dve.wait_ge(ident_ready, 1)
                dve.wait_ge(masked, k + 1)
                diag = w_in[:, k, k * P:(k + 1) * P]
                dve.tensor_tensor(diag, diag, ident[:], ALU.add).then_inc(diag_ready, 1)
                dve.wait_ge(hi_ready, k + 1)
                dve.tensor_tensor(walls[1][:, 1, k], w_in[:, k], walls[1][:, 0, k].bitcast(F32), ALU.subtract)\
                   .then_inc(lo_ready, 1)

            block_sums(0)
            compare(0)
            for k in range(KC):
                if k + 1 < KC:
                    block_sums(k + 1)
                    compare(k + 1)
                finish(k)

            done = [0]

            def after(ins):
                done[0] += 1
                ins.then_inc(dve_done, 1)
                dve.wait_ge(dve_done, done[0])

            dve.wait_ge(small_loaded, 48)
            dve.wait_ge(adapter_parts, 2)
            after(dve.tensor_reduce(win_mean[:], win_in[:], AX, ALU.add))
            after(dve.tensor_scalar(win_mean[:], win_mean[:], 1.0 / P, None, ALU.mult))
            dve.tensor_tensor(win_in[:], win_in[:], win_mean[:].unsqueeze(2).broadcast_to([P, KC, P]), ALU.subtract)\
               .then_inc(win_ready, 1)
            dve.tensor_scalar(centre[:], ident[:], -1.0 / P, None, ALU.add).then_inc(centre_ready, 1)
            for b in range(BATCHES):
                after(dve.tensor_scalar(below[:, b], starts[:], float(b), None, ALU.is_le))
            after(dve.tensor_reduce(count[:], below[:], AX, ALU.add))
            after(dve.tensor_tensor(adapter[:, 0:1], adapter[:, 0:1], adapter[:, 1:2], ALU.add))
            after(dve.tensor_scalar(adapter[:, 0:1], adapter[:, 0:1], 2.0, None, ALU.add))
            after(dve.memset(persist["coef"][:48, BATCHES:BATCHES + 1], 0.0))
            after(dve.tensor_scalar(persist["coef"][:48, 0:BATCHES], count[:], adapter[:, 0:1], None, ALU.is_equal))
            dve.wait_ge(bias_done, 1)
            after(dve.tensor_copy(persist["bias_c"][:], ps_bias[:]))
            dve.wait_ge(win_hi_ready, 1)
            after(dve.tensor_tensor(persist["win_lo"][:], win_in[:], persist["win_hi"][:].bitcast(F32), ALU.subtract))


VECS = ["phz_re", "phz_im", "lc_re", "lc_im", "sc_lin", "ln1_w", "ln1_b", "ln2_w", "ln2_b"]
LEVELS = 10


class Preparation:

    def __init__(self, nc, ctx, io, spill, ident, m):
        def sb(name, shape, dt=F32):
            return ctx.enter_context(nc.sbuf_tensor(f"T_{name}", shape, dt))

        def sem(name):
            return ctx.enter_context(nc.semaphore(f"T_{name}"))

        self.io, self.spill, self.ident, self.m = io, spill, ident, m
        self.table = sb("table", [P, 2, LAYERS, SEQ])
        self.cross = sb("cross", [P, 2, LAYERS, SEQ // 2])
        self.w1 = sb("w1", [P, LAYERS, FCH * P])
        self.w2 = sb("w2", [P, LAYERS * FCH, P])
        self.b1_in = sb("b1_in", [P, LAYERS * FCH])
        self.mix = sb("mix", [P, LAYERS, P])
        self.w2_mean = sb("w2_mean", [P, LAYERS * FCH])
        self.lnl = sb("lnl", [P, 2])
        self.wout = sb("wout", [P, D])
        self.bout = sb("bout", [ROWS, D])
        self.brow = sb("brow", [ROWS, D])
        self.centre = sb("centre", [P, P])
        self.sq_re = sb("sq_re", [P, LAYERS])
        self.sq_im = sb("sq_im", [P, LAYERS])
        self.r2 = sb("r2", [P, LAYERS])
        self.r2_safe = sb("r2_safe", [P, LAYERS])
        self.is_zero = sb("is_zero", [P, LAYERS])
        self.r_inv = sb("r_inv", [P, LAYERS])
        self.minus_half = sb("minus_half", [P, LAYERS])
        self.radius = sb("radius", [P, LAYERS])
        self.fix = sb("fix", [P, LAYERS])
        self.anchor = sb("anchor", [P, LEVELS, 2, LAYERS])
        self.ps_b1 = ctx.enter_context(nc.psum_tensor("T_ps_b1", [P, LAYERS * FCH], F32))
        self.ps_row = [ctx.enter_context(nc.psum_tensor(f"T_ps_row{h}", [ROWS, HALF], F32)) for h in range(2)]
        self.loaded = sem("loaded")
        self.const_ready = sem("const_ready")
        self.r2_ready = sem("r2_ready")
        self.r_inv_ready = sem("r_inv_ready")
        self.radius_ready = sem("radius_ready")
        self.rho_ready = sem("rho_ready")
        self.b1_product = sem("b1_product")
        self.row_product = sem("row_product")
        self.dve_done = sem("dve_done")
        self.all_ready = sem("all_ready")
        self.spilled = sem("spilled")
        self.done = 0

    def v(self, name):
        return self.m["vec"][:, VECS.index(name)]

    def load(self, sp):
        io = self.io
        sp.dma_start(self.m["vec"][:], io["vec"]).then_inc(self.loaded, 16)
        sp.dma_start(self.w1[:], io["mlp1_t"]).then_inc(self.loaded, 16)
        sp.dma_start(self.w2[:], io["mlp2_t"].rearrange("p l q d -> p (l q) d")).then_inc(self.loaded, 16)
        sp.dma_start(self.b1_in[:], io["mlp_b1"].rearrange("p l q -> p (l q)")).then_inc(self.loaded, 16)
        sp.dma_start(self.lnl[:], io["lnl"]).then_inc(self.loaded, 16)
        sp.dma_start(self.wout[:], io["wout_t"]).then_inc(self.loaded, 16)
        sp.dma_start(self.bout[:], io["bout"].partition_broadcast(ROWS)).then_inc(self.loaded, 16)

    def store(self, sp):
        spill = self.spill
        sp.wait_ge(self.all_ready, 1)
        sp.dma_start(spill["w1"], self.w1[:].rearrange("p l c -> p (l c)")).then_inc(self.spilled, 16)
        sp.dma_start(spill["w2"], self.w2[:].rearrange("p n d -> p (n d)")).then_inc(self.spilled, 16)
        sp.dma_start(spill["mix"], self.mix[:].rearrange("p l d -> p (l d)")).then_inc(self.spilled, 16)
        sp.dma_start(spill["table"], self.table[:].rearrange("p i l t -> p (i l t)")).then_inc(self.spilled, 16)
        sp.dma_start(spill["wout"], self.wout[:]).then_inc(self.spilled, 16)
        sp.dma_start(spill["brow"], self.brow[:]).then_inc(self.spilled, 16)

    def wait_stored(self, sp):
        sp.wait_ge(self.spilled, 6 * 16)

    def tensor_part(self, pe):
        pe.wait_ge(self.loaded, 7 * 16)
        for n in range(LAYERS * FCH):
            l, q = n // FCH, n % FCH
            last = pe.matmul(self.ps_b1[:, n:n + 1], self.w1[:, l, q * P:(q + 1) * P],
                             self.v("ln2_b")[:, l:l + 1], start=True, stop=True)
        last.then_inc(self.b1_product, 1)
        for h in range(2):
            last = pe.matmul(self.ps_row[h][:], self.lnl[:, 1:2].broadcast_to([P, ROWS]),
                             self.wout[:, h * HALF:(h + 1) * HALF], start=True, stop=True)
        last.then_inc(self.row_product, 1)

    def pool_part(self, pool):
        pool.memset(self.minus_half[:], -0.5).then_inc(self.const_ready, 1)
        pool.wait_ge(self.const_ready, 1)
        pool.wait_ge(self.r2_ready, 1)
        pool.tensor_tensor(self.r_inv[:], self.r2_safe[:], self.minus_half[:], ALU.pow).then_inc(self.r_inv_ready, 1)

    def scalar_part(self, act):
        act.wait_ge(self.radius_ready, 1)
        act.activation(self.m["rho"][:], self.radius[:], ACT.Tanh).then_inc(self.rho_ready, 1)

    def extend(self, dve, mark, i, level):
        n = 2 ** level
        for l in range(LAYERS):
            factor = self.anchor[:, level, i, l:l + 1]
            mark(dve.scalar_tensor_tensor(self.table[:, i, l, n:2 * n], self.table[:, 0, l, 0:n], factor,
                                          self.cross[:, i, l, 0:n], ALU.mult, (ALU.subtract, ALU.add)[i]))

    def vector_part(self, dve, j):
        def mark(ins):
            self.done += 1
            ins.then_inc(self.dve_done, 1)

        def settle():
            dve.wait_ge(self.dve_done, self.done)

        def after(ins):
            mark(ins)
            settle()

        v, fix, table, cross, anchor = self.v, self.fix, self.table, self.cross, self.anchor
        sq_re, sq_im, r2, r_inv, is_zero = self.sq_re, self.sq_im, self.r2, self.r_inv, self.is_zero
        if j == 0:
            dve.wait_ge(self.loaded, 7 * 16)
            mark(dve.tensor_tensor(sq_re[:], v("phz_re"), v("phz_re"), ALU.mult))
            after(dve.tensor_tensor(sq_im[:], v("phz_im"), v("phz_im"), ALU.mult))
            after(dve.tensor_tensor(r2[:], sq_re[:], sq_im[:], ALU.add))
            dve.tensor_scalar(self.r2_safe[:], r2[:], 1e-37, None, ALU.max).then_inc(self.r2_ready, 1)
            after(dve.tensor_scalar(is_zero[:], r2[:], 1e-30, None, ALU.is_le))
            after(dve.tensor_scalar(fix[:], is_zero[:], -1.0, 1.0, ALU.mult, ALU.add))
            dve.wait_ge(self.r_inv_ready, 1)
            dve.tensor_tensor(self.radius[:], r2[:], r_inv[:], ALU.mult).then_inc(self.radius_ready, 1)
            dve.wait_ge(self.radius_ready, 1)
            after(dve.tensor_tensor(r_inv[:], r_inv[:], fix[:], ALU.mult))
            after(dve.tensor_tensor(sq_re[:], v("phz_re"), r_inv[:], ALU.mult))
            mark(dve.tensor_tensor(anchor[:, 0, 0], sq_re[:], is_zero[:], ALU.add))
            after(dve.scalar_tensor_tensor(anchor[:, 0, 1], v("phz_im"), -1.0, r_inv[:], ALU.mult, ALU.mult))
        elif j <= LEVELS:
            level = j - 1
            c, s = anchor[:, level, 0], anchor[:, level, 1]
            if level:
                pc, ps = anchor[:, level - 1, 0], anchor[:, level - 1, 1]
                mark(dve.tensor_tensor(sq_re[:], pc, pc, ALU.mult))
                mark(dve.tensor_tensor(sq_im[:], ps, ps, ALU.mult))
                after(dve.scalar_tensor_tensor(s, pc, 2.0, ps, ALU.mult, ALU.mult))
                after(dve.tensor_tensor(c, sq_re[:], sq_im[:], ALU.subtract))
            mark(dve.tensor_tensor(sq_re[:], c, c, ALU.mult))
            after(dve.tensor_tensor(sq_im[:], s, s, ALU.mult))
            after(dve.tensor_tensor(fix[:], sq_re[:], sq_im[:], ALU.add))
            after(dve.tensor_scalar(fix[:], fix[:], -0.5, 1.5, ALU.mult, ALU.add))
            mark(dve.tensor_tensor(c, c, fix[:], ALU.mult))
            after(dve.tensor_tensor(s, s, fix[:], ALU.mult))
            if level == 0:
                for i in range(2):
                    mark(dve.tensor_copy(table[:, i, :, 0:1], anchor[:, 0, i].unsqueeze(2)))
                settle()
            n = 2 ** level
            for l in range(LAYERS):
                ac, an = anchor[:, level, 0, l:l + 1], anchor[:, level, 1, l:l + 1]
                mark(dve.tensor_scalar(cross[:, 0, l, 0:n], table[:, 1, l, 0:n], an, None, ALU.mult))
                mark(dve.tensor_scalar(cross[:, 1, l, 0:n], table[:, 1, l, 0:n], ac, None, ALU.mult))
            settle()
            self.extend(dve, mark, 0, level)
            if level < LEVELS - 1:
                self.extend(dve, mark, 1, level)
            settle()
        elif j == LEVELS + 1:
            self.extend(dve, mark, 1, LEVELS - 1)
        elif j == LEVELS + 2:
            dve.wait_ge(self.b1_product, 1)
            mark(dve.tensor_tensor(self.m["b1"][:].rearrange("p l q -> p (l q)"), self.ps_b1[:], self.b1_in[:],
                                   ALU.add))
            for l in range(LAYERS):
                mark(dve.tensor_scalar(self.w1[:, l], self.w1[:, l], v("ln2_w")[:, l:l + 1], None, ALU.mult))
        elif j == LEVELS + 3:
            after(dve.tensor_reduce(self.w2_mean[:], self.w2[:], AX, ALU.add))
            after(dve.tensor_scalar(self.w2_mean[:], self.w2_mean[:], 1.0 / P, None, ALU.mult))
            mean = self.w2_mean[:].unsqueeze(2).broadcast_to([P, LAYERS * FCH, P])
            mark(dve.tensor_tensor(self.w2[:], self.w2[:], mean, ALU.subtract))
        elif j == LEVELS + 4:
            after(dve.tensor_scalar(self.centre[:], self.ident[:], -1.0 / P, None, ALU.add))
            for l in range(LAYERS):
                mark(dve.tensor_scalar(self.mix[:, l], self.centre[:], v("sc_lin")[:, l:l + 1], None, ALU.mult))
            dve.wait_ge(self.row_product, 1)
            mark(dve.tensor_scalar(self.wout[:], self.wout[:], self.lnl[:, 0:1], None, ALU.mult))
            for h in range(2):
                cols = slice(h * HALF, (h + 1) * HALF)
                mark(dve.tensor_tensor(self.brow[:, cols], self.ps_row[h][:], self.bout[:, cols], ALU.add))
            settle()
        elif j == LEVELS + 5:
            dve.wait_ge(self.rho_ready, 1)
            settle()
            dve.memset(fix[:], 0.0).then_inc(self.all_ready, 1)


def column_variance(pe, out, squares, mean_col):
    for c in range(HALF // P):
        last = pe.matmul(out[:, c:c + 1], squares[:, c * P:(c + 1) * P], mean_col[:], start=True, stop=True)
    return last


def spread_rows(pe, out, cols, ident):
    for c in range(HALF // P):
        last = pe.transpose(out[:, c * P:(c + 1) * P], cols[:, c:c + 1].broadcast_to([P, P]), ident[:])
    return last


def small_model_phase(nc, io, ident, m):
    with ExitStack() as ctx:
        def sb(name, shape, dt=F32):
            return ctx.enter_context(nc.sbuf_tensor(f"M_{name}", shape, dt))

        def psum(name):
            return ctx.enter_context(nc.psum_tensor(f"M_{name}", [P, HALF], F32))

        def sem(name):
            return ctx.enter_context(nc.semaphore(f"M_{name}"))

        vec, table, h = m["vec"], m["table"], m["h"]
        mean_col = sb("mean_col", [P, 1])
        minus_half = sb("minus_half", [P, 4])
        squares1 = sb("squares1", [P, HALF])
        squares2 = sb("squares2", [P, HALF])
        start = sb("start", [P, 1])
        var1 = sb("var1", [P, 4])
        var2 = sb("var2", [P, 4])
        rstd1 = sb("rstd1", [P, 4])
        rstd2 = sb("rstd2", [P, 4])
        z1 = sb("z1", [P, HALF])
        x = sb("x", [P, HALF])
        x_cos = sb("x_cos", [P, HALF])
        x_sin = sb("x_sin", [P, HALF])
        u = sb("u", [P, 2, 2, HALF])
        y_cos = sb("y_cos", [P, HALF])
        y_sin = sb("y_sin", [P, HALF])
        y = sb("y", [P, HALF])
        y_hi = sb("y_hi", [P, 2, HALF], F32R)
        y_lo = sb("y_lo", [P, 2, HALF], F32R)
        z2 = sb("z2", [P, HALF])
        z2_hi = sb("z2_hi", [P, 2, HALF], F32R)
        z2_lo = sb("z2_lo", [P, 2, HALF], F32R)
        g = sb("g", [P, FCH, HALF])
        g_hi = sb("g_hi", [P, FCH, HALF], F32R)
        g_lo = sb("g_lo", [P, FCH, HALF], F32R)
        mix_hi = sb("mix_hi", [P, P], F32R)
        mix_lo = sb("mix_lo", [P, P], F32R)
        w1_hi = sb("w1_hi", [P, FCH * P], F32R)
        w1_lo = sb("w1_lo", [P, FCH * P], F32R)
        w2_hi = sb("w2_hi", [P, FCH * P], F32R)
        w2_lo = sb("w2_lo", [P, FCH * P], F32R)
        ps_r1, ps_r2, ps_mix, ps_o = psum("ps_r1"), psum("ps_r2"), psum("ps_mix"), psum("ps_o")
        ps_v1, ps_v2 = psum("ps_v1"), psum("ps_v2")
        ps_f = [psum(f"ps_f{i}") for i in range(2)]

        h_loaded = [sem(f"h_loaded{u}") for u in range(UNITS)]
        table_loaded = [sem(f"table_loaded{i}") for i in range(2)]
        weights_loaded = [sem(f"weights_loaded{i}") for i in range(2)]
        consts = sem("consts")
        h_ready = sem("h_ready")
        h_mid = sem("h_mid")
        sq1_ready, sq2_ready = sem("sq1_ready"), sem("sq2_ready")
        v1_done, v2_done = sem("v1_done"), sem("v2_done")
        var1_ready, var2_ready = sem("var1_ready"), sem("var2_ready")
        rstd1_ready, rstd2_ready = sem("rstd1_ready"), sem("rstd2_ready")
        spread1, spread2 = sem("spread1"), sem("spread2")
        z1_ready, z2_ready = sem("z1_ready"), sem("z2_ready")
        x_ready = sem("x_ready")
        x_cos_ready, x_sin_ready = sem("x_cos_ready"), sem("x_sin_ready")
        u_ready = sem("u_ready")
        y_cos_ready, y_sin_ready = sem("y_cos_ready"), sem("y_sin_ready")
        y_ready, y_hi_ready, y_lo_ready = sem("y_ready"), sem("y_hi_ready"), sem("y_lo_ready")
        mixed = sem("mixed")
        z2_hi_ready, z2_lo_ready = sem("z2_hi_ready"), sem("z2_lo_ready")
        f_done = sem("f_done")
        g_ready, g_hi_ready, g_lo_ready = sem("g_ready"), sem("g_hi_ready"), sem("g_lo_ready")
        o_done = sem("o_done")
        mix_hi_ready, mix_lo_ready = sem("mix_hi_ready"), sem("mix_lo_ready")
        w_hi_ready, w_lo_ready = sem("w_hi_ready"), sem("w_lo_ready")

        def of_layer(ap, layer):
            return ap[:, layer:layer + 1] if isinstance(layer, int) else ap[:, bass.ds(layer, 1)]

        def tokens(place):
            return slice(place * HALF, (place + 1) * HALF)

        def run(eng, stages):
            def step(turn, at):
                due = [(at - "ABCDEFG".index(stage), part) for stage, part in stages if at >= "ABCDEFG".index(stage)]
                for over, parts in groupby(due, lambda x: x[0] >= UNITS):
                    with (eng.If(turn < LAYERS - 1) if over else nullcontext()):
                        layer = (turn + 1) % LAYERS if over else turn
                        for at_unit, part in parts:
                            part(UNITS * turn + at_unit, layer, at_unit % UNITS)
            for at in range(LAG):
                step(0, at)
            with eng.Fori(0, LAYERS) as turn:
                for at in range(LAG, UNITS + LAG):
                    step(turn, at)

        def first(n, count):
            return isinstance(n, int) and n < count

        block = ctx.enter_context(nc.Block())

        @block.sync
        def _(sp):
            def load_layers(i, first, end):
                table_in = io["table"].rearrange("p (i l t) -> p i l t", i=2, l=LAYERS)
                for part in range(2):
                    sp.dma_start(table[:, part, first:end], table_in[:, part, first:end])\
                      .then_inc(table_loaded[i], 16)
                for name, size in (("mix", P), ("w1", FCH * P), ("w2", FCH * P)):
                    dst = m["w2_flat"] if name == "w2" else m[name]
                    src = io[name].rearrange("p (l c) -> p l c", l=LAYERS)
                    sp.dma_start(dst[:, first:end], src[:, first:end]).then_inc(weights_loaded[i], 16)

            for u in range(UNITS):
                sp.dma_start(h[:, tokens(u)], io["h"][:, tokens(u)]).then_inc(h_loaded[u], 16)
                if u == 0:
                    load_layers(0, 0, 1)
            load_layers(1, 1, LAYERS)

        @block.tensor
        def _(pe):
            def mix(n, layer, place):
                pe.wait_ge(y_hi_ready, n + 1)
                pe.wait_ge(y_lo_ready, n + 1)
                pe.wait_ge(h_mid, n)
                if place == 0:
                    pe.wait_ge(mix_hi_ready, n + UNITS)
                    pe.wait_ge(mix_lo_ready, n + UNITS)
                s = place % 2
                pe.matmul(ps_mix[:], mix_hi[:], y_hi[:, s], start=True, stop=False)
                pe.matmul(ps_mix[:], mix_hi[:], y_lo[:, s], start=False, stop=False)
                pe.matmul(ps_mix[:], mix_lo[:], y_hi[:, s], start=False, stop=True).then_inc(mixed, 1)

            def hidden(q):
                def part(n, layer, place):
                    if q == 0:
                        pe.wait_ge(z2_hi_ready, n + 1)
                        pe.wait_ge(z2_lo_ready, n + 1)
                        if place == 0:
                            pe.wait_ge(w_hi_ready, 2 * n + 2 * UNITS)
                            pe.wait_ge(w_lo_ready, 2 * n + 2 * UNITS)
                    if q >= 2 or not first(n, 1):
                        pe.wait_ge(g_ready, FCH * n + q - 1)
                    s = place % 2
                    cols = slice(q * P, (q + 1) * P)
                    bank = ps_f[q % 2]
                    pe.matmul(bank[:], w1_hi[:, cols], z2_hi[:, s], start=True, stop=False)
                    pe.matmul(bank[:], w1_hi[:, cols], z2_lo[:, s], start=False, stop=False)
                    pe.matmul(bank[:], w1_lo[:, cols], z2_hi[:, s], start=False, stop=True).then_inc(f_done, 1)
                return part

            def back(q):
                def part(n, layer, place):
                    pe.wait_ge(g_hi_ready, FCH * n + q + 1)
                    pe.wait_ge(g_lo_ready, FCH * n + q + 1)
                    if q == 0:
                        pe.wait_ge(h_ready, n + UNITS)
                    s = q
                    cols = slice(q * P, (q + 1) * P)
                    pe.matmul(ps_o[:], w2_hi[:, cols], g_hi[:, s], start=(q == 0), stop=False)
                    pe.matmul(ps_o[:], w2_hi[:, cols], g_lo[:, s], start=False, stop=False)
                    pe.matmul(ps_o[:], w2_lo[:, cols], g_hi[:, s], start=False, stop=(q == FCH - 1))\
                      .then_inc(o_done, 1)
                return part

            def variance1(n, layer, place):
                pe.wait_ge(sq1_ready, n + 1)
                pe.wait_ge(var1_ready, n)
                column_variance(pe, ps_v1, squares1, mean_col).then_inc(v1_done, 1)

            def variance2(n, layer, place):
                pe.wait_ge(sq2_ready, n + 1)
                pe.wait_ge(var2_ready, n)
                column_variance(pe, ps_v2, squares2, mean_col).then_inc(v2_done, 1)

            def spread_rstd1(n, layer, place):
                pe.wait_ge(rstd1_ready, n + 1)
                pe.wait_ge(z1_ready, n)
                spread_rows(pe, ps_r1, rstd1, ident).then_inc(spread1, 1)

            def spread_rstd2(n, layer, place):
                pe.wait_ge(rstd2_ready, n + 1)
                pe.wait_ge(z2_ready, n)
                spread_rows(pe, ps_r2, rstd2, ident).then_inc(spread2, 1)

            pe.wait_ge(consts, 2)
            run(pe, [("F", hidden(2)), ("D", mix), ("F", hidden(3)), ("B", spread_rstd1), ("F", back(0)),
                     ("A", variance1), ("F", back(1)), ("D", variance2), ("F", back(2)), ("F", back(3)),
                     ("E", hidden(0)), ("D", spread_rstd2), ("E", hidden(1))])

        @block.scalar
        def _(act):
            def split_y(n, layer, place):
                if place == 0:
                    act.wait_ge(mixed, n)
                elif not first(n, 2):
                    act.wait_ge(mixed, n - 1)
                if place == 0:
                    act.wait_ge(weights_loaded[0 if first(n, 1) else 1], 3 * 16)
                    src = m["mix"][:, layer] if isinstance(layer, int) else \
                        m["mix"][:, bass.ds(layer, 1)].rearrange("p a d -> p (a d)")
                    act.activation(mix_hi[:], src, ACT.Identity).then_inc(mix_hi_ready, UNITS)
                act.wait_ge(y_ready, n + 1)
                act.activation(y_hi[:, place % 2], y[:], ACT.Identity).then_inc(y_hi_ready, 1)

            def square1(n, layer, place):
                act.wait_ge(h_ready, n + 1)
                act.wait_ge(v1_done, n)
                act.wait_ge(h_loaded[place], 16)
                act.activation(squares1[:], h[:, tokens(place)], ACT.Square).then_inc(sq1_ready, 1)

            def square2(n, layer, place):
                act.wait_ge(h_mid, n + 1)
                act.wait_ge(v2_done, n)
                act.activation(squares2[:], h[:, tokens(place)], ACT.Square).then_inc(sq2_ready, 1)

            def split_weights(n, layer, place):
                if place == 0:
                    act.wait_ge(o_done, FCH * n)
                    act.wait_ge(weights_loaded[0 if first(n, 1) else 1], 3 * 16)
                    for w, w_hi in ((m["w1"], w1_hi), (m["w2_flat"], w2_hi)):
                        src = w[:, layer] if isinstance(layer, int) else \
                            w[:, bass.ds(layer, 1)].rearrange("p a d -> p (a d)")
                        act.activation(w_hi[:], src, ACT.Identity).then_inc(w_hi_ready, UNITS)

            def silu_hidden(q):
                def part(n, layer, place):
                    if not first(n, 1):
                        act.wait_ge(g_lo_ready, FCH * (n - 1) + q + 1)
                    due = act.compute_val(FCH * n + q + 1)
                    act.wait_ge(consts, 2)
                    act.wait_ge(f_done, due)
                    b1 = m["b1"][:, :, q]
                    act.activation(g[:, q], ps_f[q % 2][:], ACT.Silu, bias=of_layer(b1, layer))\
                       .then_inc(g_ready, 1)
                return part

            def split_g(q):
                def part(n, layer, place):
                    act.wait_ge(g_ready, FCH * n + q + 1)
                    if not first(n, 1):
                        act.wait_ge(o_done, FCH * (n - 1) + q + 1)
                    act.activation(g_hi[:, q], g[:, q], ACT.Identity).then_inc(g_hi_ready, 1)
                return part

            def silu_x(n, layer, place):
                due, free = act.compute_val(n + 1), act.compute_val(n)
                act.wait_ge(consts, 2)
                act.wait_ge(z1_ready, due)
                act.wait_ge(x_cos_ready, free)
                act.wait_ge(x_sin_ready, free)
                act.activation(x[:], z1[:], ACT.Silu, bias=of_layer(vec[:, VECS.index("ln1_b")], layer),
                               scale=of_layer(vec[:, VECS.index("ln1_w")], layer)).then_inc(x_ready, 1)

            def split_z2(n, layer, place):
                act.wait_ge(z2_ready, n + 1)
                if not first(n, 2):
                    act.wait_ge(f_done, FCH * (n - 1))
                act.activation(z2_hi[:, place % 2], z2[:], ACT.Identity).then_inc(z2_hi_ready, 1)

            run(act, [("B", square1), ("G", silu_hidden(2)), ("G", split_g(1)), ("G", silu_hidden(3)),
                      ("E", square2), ("G", split_g(2)), ("G", split_g(3)), ("F", split_z2), ("F", split_weights),
                      ("C", silu_x), ("D", split_y), ("F", silu_hidden(0)), ("F", split_g(0)),
                      ("F", silu_hidden(1))])

        @block.vector
        def _(dve):
            dve.memset(mean_col[:], 1.0 / P).then_inc(consts, 1)
            dve.memset(start[:], 0.0).then_inc(h_ready, UNITS)

            def split_y(n, layer, place):
                if place == 0:
                    src = m["mix"][:, layer] if isinstance(layer, int) else \
                        m["mix"][:, bass.ds(layer, 1)].rearrange("p a d -> p (a d)")
                    dve.wait_ge(mix_hi_ready, n + UNITS)
                    dve.tensor_tensor(mix_lo[:], src, mix_hi[:].bitcast(F32), ALU.subtract)\
                       .then_inc(mix_lo_ready, UNITS)
                dve.wait_ge(y_hi_ready, n + 1)
                dve.tensor_tensor(y_lo[:, place % 2], y[:], y_hi[:, place % 2].bitcast(F32), ALU.subtract)\
                   .then_inc(y_lo_ready, 1)

            def add_mixed(n, layer, place):
                dve.wait_ge(mixed, n + 1)
                dve.tensor_tensor(h[:, tokens(place)], ps_mix[:], h[:, tokens(place)], ALU.add).then_inc(h_mid, 1)

            def take_var1(n, layer, place):
                dve.wait_ge(v1_done, n + 1)
                dve.wait_ge(rstd1_ready, n)
                dve.tensor_scalar(var1[:], ps_v1[:, 0:4], EPS, None, ALU.add).then_inc(var1_ready, 1)

            def take_var2(n, layer, place):
                dve.wait_ge(v2_done, n + 1)
                dve.wait_ge(rstd2_ready, n)
                dve.tensor_scalar(var2[:], ps_v2[:, 0:4], EPS, None, ALU.add).then_inc(var2_ready, 1)

            def scan(i):
                def part(n, layer, place):
                    s = place % 2
                    dve.wait_ge((x_cos_ready, x_sin_ready)[i], n + 1)
                    dve.wait_ge(u_ready, 2 * n)
                    if i == 1 and not first(n, 2):
                        dve.wait_ge(y_sin_ready, n - 1)
                    first_state = of_layer(vec[:, VECS.index(("lc_re", "lc_im")[i])], layer) if s == 0 else \
                        u[:, 0, i, HALF - 1:HALF]
                    dve.tensor_tensor_scan(u[:, s, i], of_layer(m["rho"], layer).broadcast_to([P, HALF]),
                                           (x_cos, x_sin)[i][:], first_state, ALU.mult, ALU.add)\
                       .then_inc(u_ready, 1)
                return part

            def scale1(n, layer, place):
                dve.wait_ge(spread1, n + 1)
                dve.wait_ge(x_ready, n)
                dve.tensor_tensor(z1[:], ps_r1[:], h[:, tokens(place)], ALU.mult).then_inc(z1_ready, 1)

            def scale2(n, layer, place):
                dve.wait_ge(spread2, n + 1)
                dve.wait_ge(h_mid, n + 1)
                dve.wait_ge(z2_hi_ready, n)
                dve.tensor_tensor(z2[:], ps_r2[:], h[:, tokens(place)], ALU.mult).then_inc(z2_ready, 1)

            def split_weights(n, layer, place):
                if place == 0:
                    for i, (w, w_hi, w_lo) in enumerate(((m["w1"], w1_hi, w1_lo), (m["w2_flat"], w2_hi, w2_lo))):
                        src = w[:, layer] if isinstance(layer, int) else \
                            w[:, bass.ds(layer, 1)].rearrange("p a d -> p (a d)")
                        dve.wait_ge(w_hi_ready, 2 * n + UNITS * (i + 1))
                        dve.tensor_tensor(w_lo[:], src, w_hi[:].bitcast(F32), ALU.subtract)\
                           .then_inc(w_lo_ready, UNITS)

            def split_g(q):
                def part(n, layer, place):
                    dve.wait_ge(g_hi_ready, FCH * n + q + 1)
                    dve.tensor_tensor(g_lo[:, q], g[:, q], g_hi[:, q].bitcast(F32), ALU.subtract)\
                       .then_inc(g_lo_ready, 1)
                return part

            def split_z2(n, layer, place):
                s = place % 2
                dve.wait_ge(z2_hi_ready, n + 1)
                dve.tensor_tensor(z2_lo[:, s], z2[:], z2_hi[:, s].bitcast(F32), ALU.subtract)\
                   .then_inc(z2_lo_ready, 1)

            def add_hidden(n, layer, place):
                dve.wait_ge(o_done, FCH * (n + 1))
                dve.wait_ge(h_mid, n + 1)
                dve.scalar_tensor_tensor(h[:, tokens(place)], ps_o[:], of_layer(m["b2"], layer),
                                         h[:, tokens(place)], ALU.add, ALU.add).then_inc(h_ready, 1)

            run(dve, [("G", split_g(3)), ("B", take_var1), ("E", take_var2), ("F", split_z2), ("G", add_hidden),
                      ("F", split_weights), ("D", split_y), ("E", scale2), ("C", scan(0)), ("F", split_g(0)),
                      ("D", add_mixed), ("C", scan(1)), ("F", split_g(1)), ("B", scale1), ("F", split_g(2))])

        @block.gpsimd
        def _(pool):
            pool.memset(minus_half[:], -0.5).then_inc(consts, 1)
            pool.wait_ge(consts, 2)

            def rotate(i):
                def part(n, layer, place):
                    if place == 0 and i == 0:
                        pool.wait_ge(table_loaded[0 if first(n, 1) else 1], 2 * 16)
                    if i == 0:
                        due, free = pool.compute_val(n + 1), pool.compute_val(2 * n)
                        pool.wait_ge(consts, 2)
                        pool.wait_ge(x_ready, due)
                        pool.wait_ge(u_ready, free)
                    pool.tensor_tensor((x_cos, x_sin)[i][:], x[:], rotation(m, i, layer, place % 2), ALU.mult)\
                        .then_inc((x_cos_ready, x_sin_ready)[i], 1)
                return part

            def root1(n, layer, place):
                pool.wait_ge(var1_ready, n + 1)
                pool.wait_ge(spread1, n)
                pool.tensor_tensor(rstd1[:], var1[:], minus_half[:], ALU.pow).then_inc(rstd1_ready, 1)

            def root2(n, layer, place):
                pool.wait_ge(var2_ready, n + 1)
                pool.wait_ge(spread2, n)
                pool.tensor_tensor(rstd2[:], var2[:], minus_half[:], ALU.pow).then_inc(rstd2_ready, 1)

            def rotate_back(i):
                def part(n, layer, place):
                    s = place % 2
                    due = pool.compute_val(2 * n + 1 + i)
                    pool.wait_ge(consts, 2)
                    pool.wait_ge(u_ready, due)
                    pool.tensor_tensor((y_cos, y_sin)[i][:], u[:, s, i], rotation(m, i, layer, s), ALU.mult)\
                        .then_inc((y_cos_ready, y_sin_ready)[i], 1)
                return part

            def real_part(n, layer, place):
                pool.wait_ge(y_lo_ready, n)
                pool.wait_ge(y_cos_ready, n + 1)
                pool.wait_ge(y_sin_ready, n + 1)
                pool.tensor_tensor(y[:], y_cos[:], y_sin[:], ALU.add).then_inc(y_ready, 1)

            run(pool, [("D", rotate_back(0)), ("D", rotate_back(1)), ("D", real_part), ("E", root2),
                       ("C", rotate(0)), ("B", root1), ("C", rotate(1))])


def rotation(m, i, layer, half):
    cols = slice(half * HALF, (half + 1) * HALF)
    if isinstance(layer, int):
        return m["table"][:, i, layer, cols]
    return m["table"][:, i, bass.ds(layer, 1), cols].rearrange("p a t -> p (a t)")

def readout_phase(nc, io, ident, m, q):
    TPU = HALF // P
    SLOTS = 4
    MORE = SLOTS - 1
    with ExitStack() as ctx:
        def sb(name, shape, dt=F32):
            return ctx.enter_context(nc.sbuf_tensor(f"C_{name}", shape, dt))

        def psum(name, shape):
            return ctx.enter_context(nc.psum_tensor(f"C_{name}", shape, F32))

        def sem(name):
            return ctx.enter_context(nc.semaphore(f"C_{name}"))

        h = m["h"]
        mean_col = sb("mean_col", [P, 1])
        minus_half = sb("minus_half", [P, TPU])
        token_weight = sb("token_weight", [P, 1])
        routed = sb("routed", [P, 2])
        start = sb("start", [P, 2])
        squares = sb("squares", [P, HALF])
        var = sb("var", [P, TPU])
        z_rstd = sb("z_rstd", [P, TPU])
        z = sb("z", [P, HALF])
        z_hi = sb("z_hi", [P, 2, HALF], F32R)
        z_lo = sb("z_lo", [P, 2, HALF], F32R)
        x_in = sb("x_in", [P, SLOTS, D])
        row = sb("row", [P, SLOTS, D])
        stats = sb("stats", [P, 2, 2, 6])
        mean_var = sb("mean_var", [P, 2, 2])
        var_eps = sb("var_eps", [P, 2])
        rstd = sb("rstd", [P, 2])
        shift = sb("shift", [P, 2])
        total = sb("total", [P, D])
        last = sb("last", [P, HALF])
        ps_out = [[psum(f"ps_out{s}{i}", [P, HALF]) for i in range(2)] for s in range(2)]
        ps_var = psum("ps_var", [P, TPU])
        ps_z = psum("ps_z", [P, HALF])
        ps_q = psum("ps_q", [P, KC])

        ones = sb("ones", [ROWS, P])
        ones_rows = sb("ones_rows", [ROWS, P], F32R)
        wout = sb("wout", [P, D])
        bias_rows = sb("bias_rows", [ROWS, D])
        wout_hi = sb("wout_hi", [P, D], F32R)
        wout_lo = sb("wout_lo", [P, D], F32R)
        brow = sb("brow", [ROWS, D], F32R)

        loaded = sem("loaded")
        ones_set = sem("ones_set")
        ones_ready = sem("ones_ready")
        out_hi_ready = sem("out_hi_ready")
        out_lo_ready = sem("out_lo_ready")
        consts = sem("consts")
        squared = sem("squared")
        var_done = sem("var_done")
        var_ready = sem("var_ready")
        z_rstd_ready = sem("z_rstd_ready")
        spread = sem("spread")
        z_ready, z_hi_ready, z_lo_ready = sem("z_ready"), sem("z_hi_ready"), sem("z_lo_ready")
        x_loaded = [sem(f"x_loaded{s}") for s in range(SLOTS)]
        mm_done = sem("mm_done")
        added = sem("added")
        stats_ready, mv_ready, ve_ready = sem("stats_ready"), sem("mv_ready"), sem("ve_ready")
        rstd_ready, shift_ready = sem("rstd_ready"), sem("shift_ready")
        normed = sem("normed")
        stored = [sem(f"stored{s}") for s in range(SLOTS)]
        totalled = [sem(f"totalled{i}") for i in range(2)]
        last_ready = sem("last_ready")
        q_done = sem("q_done")
        q_taken = sem("q_taken")

        def steps(eng, step):
            with eng.Fori(0, BATCHES) as batch:
                for j in range(TPB):
                    step(batch, j)

        def before(batch):
            return (batch + (BATCHES - 1)) % BATCHES

        def earlier(eng, batch, j, part):
            if j > 0:
                part(batch, j - 1)
            else:
                with eng.If(batch > 0):
                    part(before(batch), TPB - 1)

        def next_unit(eng, batch, j, part):
            with (eng.If(batch < BATCHES - 1) if j >= TPU else nullcontext()):
                part(2 * batch + j // TPU + 1, (j // TPU + 1) % 2)

        def unit_after_next(eng, batch, j, part):
            with eng.If(batch < BATCHES - 1):
                part(2 * batch + j // TPU + 2, j // TPU)

        block = ctx.enter_context(nc.Block())

        @block.sync
        def _(sp):
            def step(batch, j):
                t = TPB * batch + j
                sp.wait_ge(added, 2 * t + 2)
                sp.dma_start(x_in[:, j % SLOTS], io["x"][t]).then_inc(x_loaded[j % SLOTS], 16)
            sp.dma_start(wout[:], io["wout"]).then_inc(loaded, 16)
            sp.dma_start(bias_rows[:], io["brow"]).then_inc(loaded, 16)
            steps(sp, step)

        @block.tensor
        def _(pe):
            def variance(n, slot):
                pe.wait_ge(squared, n + 1)
                pe.wait_ge(var_ready, n)
                column_variance(pe, ps_var, squares, mean_col).then_inc(var_done, 1)

            def spread_rstd(n, slot):
                pe.wait_ge(z_rstd_ready, n + 1)
                pe.wait_ge(z_ready, n)
                spread_rows(pe, ps_z, z_rstd, ident).then_inc(spread, 1)

            def product(t, j, i):
                pe.wait_ge(added, 2 * t + i + 1 + 2 * (SLOTS - 2))
                slot, c = j // TPU, j % TPU
                hi, lo = z_hi[:, slot, c * P:(c + 1) * P], z_lo[:, slot, c * P:(c + 1) * P]
                cols = slice(i * HALF, (i + 1) * HALF)
                bank = ps_out[j % 2][i]
                pe.matmul(bank[:], hi, wout_hi[:, cols], start=True, stop=False)
                pe.matmul(bank[:], hi, wout_lo[:, cols], start=False, stop=False)
                pe.matmul(bank[:], lo, wout_hi[:, cols], start=False, stop=False)
                pe.matmul(bank[:], ones_rows[:], brow[:, cols], start=False, stop=True).then_inc(mm_done, 1)

            def reduce_total(batch):
                pe.wait_ge(totalled[0], (TPB - 1) * (batch + 1))
                pe.wait_ge(totalled[1], (TPB - 1) * (batch + 1) + MORE)
                for k in range(KC):
                    last = pe.matmul(ps_q[:, k:k + 1], total[:, k * P:(k + 1) * P], token_weight[:],
                                     start=True, stop=True)
                last.then_inc(q_done, 1)

            pe.wait_ge(consts, 4)
            variance(0, 0)
            spread_rstd(0, 0)
            variance(1, 1)
            pe.wait_ge(out_hi_ready, 2)
            pe.wait_ge(out_lo_ready, 2)
            pe.wait_ge(ones_ready, 1)

            def step(batch, j):
                t = TPB * batch + j
                if j % TPU == 0:
                    pe.wait_ge(z_hi_ready, 2 * batch + j // TPU + 1)
                    pe.wait_ge(z_lo_ready, 2 * batch + j // TPU + 1)
                product(t, j, 0)
                if j % TPU == 0:
                    next_unit(pe, batch, j, spread_rstd)
                product(t, j, 1)
                if j == 2:
                    with pe.If(batch > 0):
                        reduce_total(before(batch))
                if j % TPU == 1:
                    unit_after_next(pe, batch, j, variance)
            steps(pe, step)
            reduce_total(BATCHES - 1)

        @block.scalar
        def _(act):
            def square(n, slot):
                act.wait_ge(var_done, n)
                tokens = h[:, HALF * n:HALF * (n + 1)] if isinstance(n, int) else \
                    h[:, bass.ds(HALF * (n % UNITS), HALF)]
                act.activation(squares[:], tokens, ACT.Square).then_inc(squared, 1)

            def split_z(n, slot):
                if not isinstance(n, int):
                    act.wait_ge(mm_done, 2 * TPU * (n - 1))
                act.wait_ge(z_ready, n + 1)
                act.activation(z_hi[:, slot], z[:], ACT.Identity).then_inc(z_hi_ready, 1)

            def normalise(batch, j):
                s, r = j % 2, j % SLOTS
                act.wait_ge(shift_ready, TPB * batch + j + 1)
                act.activation(row[:, r], row[:, r], ACT.Identity, bias=shift[:, s:s + 1],
                               scale=rstd[:, s:s + 1]).then_inc(normed, 1)
                act.wait_ge(normed, TPB * batch + j + 1)
                act.dma_start(io["out"][TPB * batch + j], row[:, r]).then_inc(stored[r], 16)

            square(0, 0)
            act.wait_ge(loaded, 2 * 16)
            act.activation(wout_hi[:], wout[:], ACT.Identity).then_inc(out_hi_ready, 1)
            act.activation(brow[:], bias_rows[:], ACT.Identity).then_inc(out_hi_ready, 1)
            split_z(0, 0)
            square(1, 1)

            def step(batch, j):
                if j % TPU == 0:
                    unit_after_next(act, batch, j, square)
                    next_unit(act, batch, j, split_z)
                earlier(act, batch, j, normalise)
            steps(act, step)
            normalise(BATCHES - 1, TPB - 1)
            for r in range(SLOTS):
                act.wait_ge(stored[r], 16 * TILES // SLOTS)

        @block.vector
        def _(dve):
            dve.memset(mean_col[:], 1.0 / P).then_inc(consts, 1)
            dve.memset(start[:, 0:1], 0.0).then_inc(added, 2 * SLOTS)
            dve.memset(start[:, 1:2], 0.0).then_inc(totalled[1], MORE)

            dve.memset(ones[:], 0.0).then_inc(ones_set, 1)
            dve.wait_ge(ones_set, 1)
            dve.memset(ones[0:1], 1.0).then_inc(ones_set, 1)
            dve.memset(ones[ROWS - 1:ROWS], 1.0).then_inc(ones_set, 1)
            dve.wait_ge(ones_set, 3)
            dve.tensor_copy(ones_rows[:], ones[:]).then_inc(ones_ready, 1)

            def take_var(n, slot):
                dve.wait_ge(var_done, n + 1)
                dve.wait_ge(z_rstd_ready, n)
                dve.tensor_scalar(var[:], ps_var[:], EPS, None, ALU.add).then_inc(var_ready, 1)

            def scale(n, slot):
                dve.wait_ge(spread, n + 1)
                dve.wait_ge(z_hi_ready, n)
                tokens = h[:, 0:HALF] if isinstance(n, int) else h[:, bass.ds(HALF * (n % UNITS), HALF)]
                dve.tensor_tensor(z[:], ps_z[:], tokens, ALU.mult).then_inc(z_ready, 1)

            def split_z(n, slot):
                dve.wait_ge(z_hi_ready, n + 1)
                dve.tensor_tensor(z_lo[:, slot], z[:], z_hi[:, slot].bitcast(F32), ALU.subtract)\
                   .then_inc(z_lo_ready, 1)

            def add_x(batch, j, i):
                t = TPB * batch + j
                s, r = j % 2, j % SLOTS
                cols = slice(i * HALF, (i + 1) * HALF)
                if i == 0:
                    dve.wait_ge(x_loaded[r], 16 * (TPB // SLOTS * batch + j // SLOTS + 1))
                    dve.wait_ge(stored[r], 16 * (TPB // SLOTS * batch + j // SLOTS))
                    dve.wait_ge(totalled[1], (TPB - 1) * batch + j - (1 if j >= SLOTS else 0))
                dve.wait_ge(mm_done, 2 * t + i + 1)
                dve.tensor_tensor(row[:, r, cols], ps_out[s][i][:], x_in[:, r, cols], ALU.add).then_inc(added, 1)

            def half_stats(batch, j, i):
                dve.wait_ge(added, 2 * (TPB * batch + j) + i + 1 + 2 * SLOTS)
                dve.bn_stats(stats[:, j % 2, i], row[:, j % SLOTS, i * HALF:(i + 1) * HALF]).then_inc(stats_ready, 1)

            def aggregate(batch, j):
                due = dve.compute_val(2 * (TPB * batch + j) + 2)
                dve.wait_ge(consts, 4)
                dve.wait_ge(stats_ready, due)
                dve.bn_aggr(mean_var[:, j % 2], stats[:, j % 2].rearrange("p a b -> p (a b)")).then_inc(mv_ready, 1)

            def add_up(batch, j):
                if j == 0:
                    return
                part, sum_so_far = row[:, j % SLOTS, :HALF], total[:, :HALF]
                dve.wait_ge(normed, TPB * batch + j + 1)
                if j == 1:
                    dve.wait_ge(q_done, batch)
                    dve.tensor_scalar(sum_so_far, part, routed[:, 0:1], None, ALU.mult).then_inc(totalled[0], 1)
                    return
                dve.wait_ge(totalled[0], (TPB - 1) * batch + j - 1)
                if j == TPB - 1:
                    dve.scalar_tensor_tensor(sum_so_far, part, routed[:, 1:2], sum_so_far, ALU.mult, ALU.add)\
                       .then_inc(totalled[0], 1)
                else:
                    dve.tensor_tensor(sum_so_far, part, sum_so_far, ALU.add).then_inc(totalled[0], 1)

            def take_q(batch):
                dve.wait_ge(q_done, batch + 1)
                column = q[:, :, batch:batch + 1] if isinstance(batch, int) else q[:, :, bass.ds(batch, 1)]
                dve.tensor_copy(column, ps_q[:].unsqueeze(2)).then_inc(q_taken, 1)

            take_var(0, 0)
            dve.wait_ge(out_hi_ready, 2)
            dve.tensor_tensor(wout_lo[:], wout[:], wout_hi[:].bitcast(F32), ALU.subtract).then_inc(out_lo_ready, 1)
            dve.tensor_tensor(brow[ROWS - 1:ROWS], bias_rows[ROWS - 1:ROWS], brow[ROWS - 1:ROWS].bitcast(F32),
                              ALU.subtract).then_inc(out_lo_ready, 1)
            scale(0, 0)
            split_z(0, 0)
            take_var(1, 1)

            def step(batch, j):
                if j % TPU == 2:
                    unit_after_next(dve, batch, j, take_var)
                add_x(batch, j, 0)
                if j % TPU == 0:
                    next_unit(dve, batch, j, scale)
                add_x(batch, j, 1)
                half_stats(batch, j, 0)
                half_stats(batch, j, 1)
                if j == 2:
                    with dve.If(batch > 0):
                        take_q(before(batch))
                earlier(dve, batch, j, add_up)
                if j % TPU == 0:
                    next_unit(dve, batch, j, split_z)
                aggregate(batch, j)
            steps(dve, step)
            add_up(BATCHES - 1, TPB - 1)
            take_q(BATCHES - 1)

        @block.gpsimd
        def _(pool):
            pool.memset(minus_half[:], -0.5).then_inc(consts, 1)
            pool.memset(token_weight[:], 1.0 / (ROUTED_END - ROUTED_START)).then_inc(consts, 1)
            pool.memset(routed[:], 1.0).then_inc(consts, 1)
            pool.wait_ge(consts, 4)
            pool.affine_select(out=routed[:, 0:1], in_=routed[:, 0:1], compare_op=ALU.is_ge, fill=0.0,
                               base=P - ROUTED_START, pattern=[[0, 1]], channel_multiplier=1)
            pool.affine_select(out=routed[:, 1:2], in_=routed[:, 1:2], compare_op=ALU.is_ge, fill=0.0,
                               base=ROUTED_END - 1 - (TPB - 1) * P, pattern=[[0, 1]], channel_multiplier=-1)\
                .then_inc(consts, 1)

            def root(n, slot):
                pool.wait_ge(var_ready, n + 1)
                pool.wait_ge(spread, n)
                pool.tensor_tensor(z_rstd[:], var[:], minus_half[:], ALU.pow).then_inc(z_rstd_ready, 1)

            def add_up(batch, j):
                if j == 0:
                    return
                part, sum_so_far = row[:, j % SLOTS, HALF:], total[:, HALF:]
                due = pool.compute_val(TPB * batch + j + 1)
                free = pool.compute_val(batch * 1)
                pool.wait_ge(consts, 4)
                pool.wait_ge(normed, due)
                if j == 1:
                    pool.wait_ge(q_done, free)
                    pool.tensor_scalar(sum_so_far, part, routed[:, 0:1], 1.0, ALU.mult, ALU.mult)\
                        .then_inc(totalled[1], 1)
                    return
                if j == TPB - 1:
                    pool.tensor_scalar(last[:], part, routed[:, 1:2], 1.0, ALU.mult, ALU.mult).then_inc(last_ready, 1)
                    pool.wait_ge(last_ready, batch + 1)
                    part = last[:]
                pool.wait_ge(totalled[1], (TPB - 1) * batch + j - 1 + MORE)
                pool.tensor_tensor(sum_so_far, part, sum_so_far, ALU.add).then_inc(totalled[1], 1)

            root(0, 0)
            root(1, 1)

            def step(batch, j):
                t = TPB * batch + j
                s = j % 2
                if j % TPU == 2:
                    unit_after_next(pool, batch, j, root)
                due = pool.compute_val(t + 1)
                pool.wait_ge(consts, 4)
                pool.wait_ge(mv_ready, due)
                pool.tensor_scalar(var_eps[:, s:s + 1], mean_var[:, s, 1:2], EPS, 1.0, ALU.add, ALU.mult)\
                    .then_inc(ve_ready, 1)
                pool.wait_ge(ve_ready, t + 1)
                pool.tensor_tensor(rstd[:, s:s + 1], var_eps[:, s:s + 1], minus_half[:, 0:1], ALU.pow)\
                    .then_inc(rstd_ready, 1)
                pool.wait_ge(consts, 4)
                pool.wait_ge(rstd_ready, due)
                pool.tensor_scalar(shift[:, s:s + 1], mean_var[:, s, 0:1], rstd[:, s:s + 1], -1.0,
                                   ALU.mult, ALU.mult).then_inc(shift_ready, 1)
                earlier(pool, batch, j, add_up)
            steps(pool, step)
            add_up(BATCHES - 1, TPB - 1)


class Router:

    def __init__(self, nc, ctx, io, ident, q, coef):
        def sb(name, shape, dt=F32):
            return ctx.enter_context(nc.sbuf_tensor(f"R_{name}", shape, dt))

        def sem(name):
            return ctx.enter_context(nc.semaphore(f"R_{name}"))

        self.io, self.ident, self.q, self.coef = io, ident, q, coef
        self.rw = sb("rw", [P, KC, EXPERTS])
        self.rb = sb("rb", [BATCHES, EXPERTS])
        self.logits = sb("logits", [BATCHES, EXPERTS])
        self.top = sb("top", [BATCHES, 1])
        self.weight = sb("weight", [BATCHES, EXPERTS])
        self.norm = sb("norm", [BATCHES, 1])
        self.wide = sb("wide", [BATCHES, EXPERTS, P // EXPERTS])
        self.ps_l = ctx.enter_context(nc.psum_tensor("R_ps_l", [BATCHES, EXPERTS], F32))
        self.ps_c = ctx.enter_context(nc.psum_tensor("R_ps_c", [P, BATCHES], F32))
        self.loaded = sem("loaded")
        self.product = sem("product")
        self.dve_done = sem("dve_done")
        self.shifted = sem("shifted")
        self.exp_done = sem("exp_done")
        self.wide_ready = sem("wide_ready")
        self.turned = sem("turned")
        self.coef_ready = sem("coef_ready")

    def load(self, sp):
        sp.dma_start(self.rw[:], self.io["rw"]).then_inc(self.loaded, 16)
        sp.dma_start(self.rb[:], self.io["rb"].partition_broadcast(BATCHES)).then_inc(self.loaded, 16)

    def tensor_part(self, pe):
        pe.wait_ge(self.loaded, 32)
        for k in range(KC):
            last = pe.matmul(self.ps_l[:], self.q[:, k], self.rw[:, k], start=(k == 0), stop=(k == KC - 1))
        last.then_inc(self.product, 1)
        pe.wait_ge(self.wide_ready, 1)
        pe.transpose(self.ps_c[:], self.wide[:].rearrange("b e r -> b (e r)"), self.ident[:BATCHES, :BATCHES])\
          .then_inc(self.turned, 1)

    def scalar_part(self, act):
        act.wait_ge(self.shifted, 1)
        act.activation(self.weight[:], self.logits[:], ACT.Exp).then_inc(self.exp_done, 1)

    def vector_part(self, dve):
        done = [0]

        def after(ins):
            done[0] += 1
            ins.then_inc(self.dve_done, 1)
            dve.wait_ge(self.dve_done, done[0])

        logits, weight, norm = self.logits, self.weight, self.norm
        after(dve.memset(self.coef[:, BATCHES:BATCHES + 1], 0.0))
        dve.wait_ge(self.loaded, 32)
        dve.wait_ge(self.product, 1)
        after(dve.tensor_tensor(logits[:], self.ps_l[:], self.rb[:], ALU.add))
        after(dve.tensor_reduce(self.top[:], logits[:], AX, ALU.max))
        dve.tensor_scalar(logits[:], logits[:], self.top[:], None, ALU.subtract).then_inc(self.shifted, 1)
        dve.wait_ge(self.exp_done, 1)
        after(dve.tensor_reduce(norm[:], weight[:], AX, ALU.add))
        after(dve.reciprocal(norm[:], norm[:]))
        after(dve.tensor_scalar(weight[:], weight[:], norm[:], ROUTER_SCALE, ALU.mult, ALU.mult))
        dve.tensor_copy(self.wide[:], weight[:].unsqueeze(2).broadcast_to([BATCHES, EXPERTS, P // EXPERTS]))\
           .then_inc(self.wide_ready, 1)
        dve.wait_ge(self.turned, 1)
        dve.tensor_copy(self.coef[:, 0:BATCHES], self.ps_c[:]).then_inc(self.coef_ready, 1)
        dve.wait_ge(self.coef_ready, 1)


def recycle_phase(nc, numbers):
    with nc.Block() as block:
        @block.gpsimd
        def _(pool):
            pool.sem_clear(range(min(numbers), max(numbers) + 1))


def build(nc, a, out):
    semaphores = list(nc.free_semaphores)
    def scratch(name, shape):
        return nc.dram_tensor(name, shape, F32, kind="Internal").ap()

    x1 = scratch("x1_scratch", (TILES, P, D))
    x2 = scratch("x2_scratch", (TILES, P, D))
    x3 = scratch("x3_scratch", (TILES, P, D))
    h0 = scratch("h0_scratch", (P, TILES * P))
    spill = {"table": scratch("table_scratch", (P, 2 * LAYERS * SEQ)),
             "w1": scratch("w1_scratch", (P, LAYERS * FCH * P)), "w2": scratch("w2_scratch", (P, LAYERS * FCH * P)),
             "mix": scratch("mix_scratch", (P, LAYERS * P)), "wout": scratch("wout_scratch", (P, D)),
             "brow": scratch("brow_scratch", (ROWS, D))}
    with ExitStack() as ctx:
        def sb(name, shape, dt=F32):
            return ctx.enter_context(nc.sbuf_tensor(name, shape, dt))

        ident = sb("ident", [P, P])
        coef = sb("coef", [P, BATCHES + 1])
        bias_c = sb("bias_c", [P, LAYERS + 1])
        m = {"vec": sb("vec", [P, len(VECS), LAYERS]), "rho": sb("rho", [P, LAYERS]),
             "b1": sb("b1", [P, LAYERS, FCH]), "b2": bias_c[:, 1:]}
        with ExitStack() as first:
            win_hi = first.enter_context(nc.sbuf_tensor("win_hi", [P, KC, P], F32R))
            win_lo = first.enter_context(nc.sbuf_tensor("win_lo", [P, KC, P], F32R))
            wall1 = first.enter_context(nc.sbuf_tensor("wall1", [P, 2, KC, D], F32R))
            persist = {"win_hi": win_hi, "win_lo": win_lo, "coef": coef, "bias_c": bias_c}
            setup_phase(nc, a, [None, wall1], ident, persist)
            with ExitStack() as beside:
                prepare = Preparation(nc, beside, a, spill, ident, m)
                dense_phase(nc, "A", {"x": a["x_t"], "out": x1}, [None, wall1], ident, prepare)
            wall0 = first.enter_context(nc.sbuf_tensor("wall0", [P, 2, KC, D], F32R))
            dense_phase(nc, "B", {"x": x1, "out": x2, "w": a["w1_t"], "bias": a["bias1"], "rank": 48,
                                  "a": a["lora_a"], "b_t": a["lora_bt"], "coef": coef[:48], "win_hi": win_hi,
                                  "win_lo": win_lo, "bin": bias_c[:, 0:1], "h": h0}, [wall0, wall1], ident)
        recycle_phase(nc, semaphores)
        q = sb("q", [P, KC, BATCHES])
        with ExitStack() as second:
            def sb1(name, shape, dt=F32):
                return second.enter_context(nc.sbuf_tensor(name, shape, dt))

            m["h"] = sb1("h", [P, TILES * P])
            with ExitStack() as small:
                def sb2(name, shape, dt=F32):
                    return small.enter_context(nc.sbuf_tensor(name, shape, dt))

                m["w1"] = sb2("w1", [P, LAYERS, FCH * P])
                m["w2_flat"] = sb2("w2", [P, LAYERS, FCH * P])
                m["mix"] = sb2("mix", [P, LAYERS, P])
                m["table"] = sb2("table", [P, 2, LAYERS, SEQ])
                small_model_phase(nc, {"h": h0, **spill}, ident, m)
            readout_phase(nc, {"x": x2, "out": x3, **spill}, ident, m, q)
        with ExitStack() as third:
            walls = [third.enter_context(nc.sbuf_tensor(f"wall_d{i}", [P, 2, KC, D], F32R)) for i in range(2)]
            router = Router(nc, third, {"rw": a["router_w"], "rb": a["router_b"]}, ident, q, coef)
            dense_phase(nc, "D", {"x": x3, "out": out, "w": a["w3_t"], "bias": a["bias3"], "rank": P,
                                  "a": a["expert_a"], "b_t": a["expert_bt"], "coef": coef}, walls, ident,
                        router=router)


def kernel(**inputs):
    import numpy as np
    import concourse.bacc as bacc
    from concourse.bass_utils import run_bass_kernel_spmd as run

    def arr(name):
        return np.asarray(inputs[name])

    laid = {
        "x_t": arr("L0_attn_data").reshape(TILES, P, KC, P).transpose(0, 3, 2, 1).reshape(TILES, P, D),
        "w0_t": arr("L0_attn_weight").T.reshape(KC, P, D),
        "mask_t": arr("L0_attn_mask").T.reshape(KC, P, D),
        "w1_t": arr("L0_ffn_weight").T.reshape(KC, P, D),
        "bias1": arr("L0_ffn_bias"),
        "lora_a": arr("L0_ffn_lora_A").reshape(48, D),
        "lora_bt": arr("L0_ffn_lora_B").transpose(0, 2, 1).reshape(48, D),
        "starts": arr("L0_ffn_lora_start_indices"),
        "win_t": arr("L1_attn_Win").T.reshape(KC, P, P).transpose(1, 0, 2),
        "vec": np.stack([arr(f"L1_attn_{n}").T for n in VECS], axis=1),
        "mlp1_t": arr("L1_attn_W1").transpose(2, 0, 1),
        "mlp2_t": arr("L1_attn_W2").reshape(LAYERS, P, FCH, P).transpose(3, 0, 2, 1),
        "mlp_b1": arr("L1_attn_b1").reshape(LAYERS, FCH, P).transpose(2, 0, 1),
        "lnl": np.stack([arr("L1_attn_lnl_w"), arr("L1_attn_lnl_b")], axis=1),
        "wout_t": arr("L1_attn_Wout").T,
        "bout": arr("L1_attn_bout"),
        "router_w": arr("L1_ffn_router_W").T.reshape(KC, P, EXPERTS).transpose(1, 0, 2),
        "router_b": arr("L1_ffn_router_b"),
        "w3_t": arr("L1_ffn_W").T.reshape(KC, P, D),
        "bias3": arr("L1_ffn_b"),
        "expert_a": arr("L1_ffn_A").reshape(P, D),
        "expert_bt": arr("L1_ffn_B").transpose(0, 2, 1).reshape(P, D),
        "bias_stack": np.concatenate([arr("L1_attn_bin")[:, None], arr("L1_attn_b2").T], axis=1),
    }
    nc = bacc.Bacc("TRN2", target_bir_lowering=False, num_devices=1)
    arrays, a = {}, {}
    for name, x in laid.items():
        arrays[f"in_{name}"] = np.ascontiguousarray(x)
        a[name] = nc.dram_tensor(f"in_{name}", x.shape, mybir.dt.from_np(x.dtype), kind="ExternalInput").ap()
    out = nc.dram_tensor("out_0", (TILES, P, D), F32, kind="ExternalOutput").ap()
    build(nc, a, out)
    r = run(nc, [arrays], core_ids=[0])
    return r.results[0]["out_0"].reshape(BATCHES, SEQ, D)
```
